# Optimizing a Trainium2 kernel written in Bass

```python
import numpy as np
import jax
import jax.numpy as jnp

def _softmax(x, axis=-1):
    return jax.nn.softmax(x, axis=axis)

def _gelu(x):
    return jax.nn.gelu(x, approximate=True)

def _silu(x):
    return jax.nn.silu(x)

def _sigmoid(x):
    return jax.nn.sigmoid(x)

def _layernorm(x, axis=-1, eps=1e-05):
    m = jnp.mean(x, axis=axis, keepdims=True)
    v = jnp.var(x, axis=axis, keepdims=True)
    return (x - m) / jnp.sqrt(v + eps)

def _scatter_add(tgt, idx, src, axis=0):
    return tgt.at[idx].add(src)

def _segment_sum(src, seg, n):
    return jax.ops.segment_sum(src, seg, n)
kernel_name = 'mk_gnn_preln_d4_gnn_r8_8cf179'

def setup_inputs(seed: int=0):
    np.random.seed(seed)
    _w = jnp.asarray

    def _rec_inputs():
        import jax
        import jax.numpy as jnp
        _gk = jax.random.key(seed)
        x = -0.000202 + 1 * jax.random.normal(jax.random.fold_in(_gk, 1), (12500, 64), jnp.float32)
        _s = jax.random.randint(jax.random.fold_in(_gk, 2), (100000,), 0, 12500, jnp.int32)
        _d = jax.random.randint(jax.random.fold_in(_gk, 3), (100000,), 0, 12500, jnp.int32)
        _loop = jnp.arange(12500, dtype=jnp.int32)
        src = jnp.concatenate([_s, _d, _loop])
        dst = jnp.concatenate([_d, _s, _loop])
        _o = jnp.argsort(dst, stable=True)
        src = src[_o]
        dst = dst[_o]
        edge_attr_16 = 0.000312547 + 1.00004 * jax.random.normal(jax.random.fold_in(_gk, 12), (212500, 16), jnp.float32)
        return (x, src, dst, edge_attr_16)
    x, src, dst, edge_attr_16 = _rec_inputs()

    def _L0_gnn_setup():
        import jax, jax.numpy as jnp
        import numpy as np
        N_NODES = 12500
        N_EDGES = 156250
        IN_C, HID_C, OUT_C = (64, 128, 64)

        def _sage_conv(x, src, dst, W_l, b_l, W_r):
            agg = jax.ops.segment_sum(x[src], dst, num_segments=N_NODES)
            deg = jax.ops.segment_sum(jnp.ones((src.shape[0],), x.dtype), dst, num_segments=N_NODES)
            mean = agg / jnp.maximum(deg, 1.0)[:, None]
            return mean @ W_l + b_l + x @ W_r
        key = jax.random.key(seed)
        ks = jax.random.split(key, 9)
        x = jax.random.normal(ks[0], (N_NODES, IN_C), dtype=jnp.float32)
        edge_index = jax.random.randint(ks[1], (2, N_EDGES), 0, N_NODES, dtype=jnp.int64)
        s = 0.1
        return {'x': x, 'edge_index': edge_index, 'W_l0': jax.random.normal(ks[2], (IN_C, HID_C), dtype=jnp.float32) * s, 'W_r0': jax.random.normal(ks[3], (IN_C, HID_C), dtype=jnp.float32) * s, 'b_l0': jnp.zeros((HID_C,), dtype=jnp.float32), 'W_l1': jax.random.normal(ks[4], (HID_C, HID_C), dtype=jnp.float32) * s, 'W_r1': jax.random.normal(ks[5], (HID_C, HID_C), dtype=jnp.float32) * s, 'b_l1': jnp.zeros((HID_C,), dtype=jnp.float32), 'W_out': jax.random.normal(ks[6], (HID_C, OUT_C), dtype=jnp.float32) * s, 'b_out': jnp.zeros((OUT_C,), dtype=jnp.float32)}
    _L0_gnn_all = _L0_gnn_setup()
    _L0_gnn_in = {k: v for k, v in _L0_gnn_all.items() if k in ('W_l0', 'W_r0', 'b_l0', 'W_l1', 'W_r1', 'b_l1', 'W_out', 'b_out')}
    del _L0_gnn_all

    def _L1_gnn_setup():
        import jax, jax.numpy as jnp
        import numpy as np
        D = 4
        H = 16
        N = 6250
        E = 100000
        TI, TJ = np.tril_indices(D, -1)

        def _householder(params):
            A = jnp.zeros(params.shape[:-1] + (D, D), params.dtype)
            A = A.at[..., TI, TJ].set(params) + jnp.eye(D, dtype=params.dtype)
            Q, R = jnp.linalg.qr(A)
            s = jnp.sign(jnp.diagonal(R, axis1=-2, axis2=-1))
            s = jnp.where(s == 0, jnp.ones_like(s), s)
            return Q * s[..., None, :]

        def _mlp(z, w1, b1, w2, b2):
            h = jax.nn.relu(z @ w1.T + b1)
            return h @ w2.T + b2

        def _forward(x, edge_index, W1, W2, epsilons, mlp1_w, mlp1_b, mlp2_w, mlp2_b):
            n = x.shape[0]
            xr = x.reshape(n, D, H)
            xt = jnp.einsum('ndf,dk->nkf', xr, W1)
            xt = jnp.einsum('ndf,fg->ndg', xt, W2)
            loops = jnp.arange(n)
            row = jnp.concatenate([edge_index[0], loops])
            col = jnp.concatenate([edge_index[1], loops])
            deg = jax.ops.segment_sum(jnp.ones_like(row, x.dtype), row, num_segments=n)
            dis = jnp.where(deg > 0, deg ** (-0.5), jnp.zeros_like(deg))
            xf = xt.reshape(n, D * H)
            xi = xf[col]
            xj = xf[row]
            cat_ve = jnp.concatenate([xi, xj], axis=-1)
            cat_ue = jnp.concatenate([xj, xi], axis=-1)
            Fve = _householder(_mlp(cat_ve, mlp1_w, mlp1_b, mlp2_w, mlp2_b))
            Fue = _householder(_mlp(cat_ue, mlp1_w, mlp1_b, mlp2_w, mlp2_b))
            xjr = xj.reshape(-1, D, H)
            msg = jnp.einsum('eka,ekb,ebh->eah', Fve, Fue, xjr)
            msg = msg * (dis[col] * dis[row])[:, None, None]
            agg = jax.ops.segment_sum(msg.reshape(-1, D * H), col, num_segments=n)
            lap = jax.nn.elu(agg.reshape(n, D, H))
            coeff = (1.0 + jnp.tanh(epsilons))[None, :, None]
            return (coeff * xr - lap).reshape(n, D * H)
        key = jax.random.key(seed)
        ks = jax.random.split(key, 9)
        dh = D * H
        x = jax.random.normal(ks[0], (N, dh), jnp.float32)
        edge_index = jax.random.randint(ks[1], (2, E), 0, N, dtype=jnp.int64)
        W1 = jax.random.normal(ks[2], (D, D), jnp.float32) / np.sqrt(D)
        W2 = jax.random.normal(ks[3], (H, H), jnp.float32) / np.sqrt(H)
        epsilons = jnp.zeros((D,), jnp.float32)
        mlp1_w = jax.random.normal(ks[4], (H, 2 * dh), jnp.float32) / np.sqrt(2 * dh)
        mlp1_b = jnp.zeros((H,), jnp.float32)
        n_params = D * (D - 1) // 2
        mlp2_w = jax.random.normal(ks[5], (n_params, H), jnp.float32) / np.sqrt(H)
        mlp2_b = jnp.zeros((n_params,), jnp.float32)
        return {'x': x, 'edge_index': edge_index, 'W1': W1, 'W2': W2, 'epsilons': epsilons, 'mlp1_w': mlp1_w, 'mlp1_b': mlp1_b, 'mlp2_w': mlp2_w, 'mlp2_b': mlp2_b}
    _L1_gnn_all = _L1_gnn_setup()
    _L1_gnn_in = {k: v for k, v in _L1_gnn_all.items() if k in ('W1', 'W2', 'epsilons', 'mlp1_w', 'mlp1_b', 'mlp2_w', 'mlp2_b')}
    del _L1_gnn_all

    def _L2_gnn_setup():
        import jax, jax.numpy as jnp
        import numpy as np
        V = 12500
        E = 200000
        C_IN = 64
        C_OUT = 64
        key = jax.random.key(seed)
        k1, k2, k3, k4, k5 = jax.random.split(key, 5)
        features = jax.random.normal(k1, (V, C_IN), dtype=jnp.float32)
        src = jax.random.randint(k2, (E,), 0, V, dtype=jnp.int32)
        tgt = jnp.sort(jax.random.randint(k3, (E,), 0, V, dtype=jnp.int32))
        W = jax.random.normal(k4, (C_OUT, 2 * C_IN), dtype=jnp.float32) * (1.0 / np.sqrt(2 * C_IN))
        b = jax.random.normal(k5, (C_OUT,), dtype=jnp.float32) * 0.01
        return {'features': features, 'src': src, 'tgt': tgt, 'W': W, 'b': b}
    _L2_gnn_all = _L2_gnn_setup()
    _L2_gnn_in = {k: v for k, v in _L2_gnn_all.items() if k in ('W', 'b')}
    del _L2_gnn_all

    def _L3_gnn_setup():
        import jax, jax.numpy as jnp
        import numpy as np
        N_NODES = 6250
        N_EDGES = 125000
        IN_SIZE = 64
        OUT_SIZE = 64
        EDGE_DIM = 16
        BN_EPS = 1e-05
        GIN_EPS = 0.0
        key = jax.random.key(seed)
        ks = jax.random.split(key, 10)
        s = 1.0 / np.sqrt(IN_SIZE)
        return {'x': jax.random.normal(ks[0], (N_NODES, IN_SIZE), dtype=jnp.float32), 'edge_index': jax.random.randint(ks[1], (2, N_EDGES), 0, N_NODES, dtype=jnp.int64), 'edge_attr': jax.random.normal(ks[2], (N_EDGES, EDGE_DIM), dtype=jnp.float32), 'W_edge': jax.random.uniform(ks[3], (IN_SIZE, EDGE_DIM), jnp.float32, -s, s), 'b_edge': jnp.zeros((IN_SIZE,), jnp.float32), 'W1': jax.random.uniform(ks[4], (OUT_SIZE, IN_SIZE), jnp.float32, -s, s), 'b1': jnp.zeros((OUT_SIZE,), jnp.float32), 'gamma': jnp.ones((OUT_SIZE,), jnp.float32), 'beta': jnp.zeros((OUT_SIZE,), jnp.float32), 'W2': jax.random.uniform(ks[5], (OUT_SIZE, OUT_SIZE), jnp.float32, -1.0 / np.sqrt(OUT_SIZE), 1.0 / np.sqrt(OUT_SIZE)), 'b2': jnp.zeros((OUT_SIZE,), jnp.float32)}
    _L3_gnn_all = _L3_gnn_setup()
    _L3_gnn_in = {k: v for k, v in _L3_gnn_all.items() if k in ('W_edge', 'b_edge', 'W1', 'b1', 'gamma', 'beta', 'W2', 'b2')}
    del _L3_gnn_all
    return {'x': x, 'src': src, 'dst': dst, 'edge_attr_16': edge_attr_16, 'L0_gnn_W_l0': _L0_gnn_in['W_l0'], 'L0_gnn_W_r0': _L0_gnn_in['W_r0'], 'L0_gnn_b_l0': _L0_gnn_in['b_l0'], 'L0_gnn_W_l1': _L0_gnn_in['W_l1'], 'L0_gnn_W_r1': _L0_gnn_in['W_r1'], 'L0_gnn_b_l1': _L0_gnn_in['b_l1'], 'L0_gnn_W_out': _L0_gnn_in['W_out'], 'L0_gnn_b_out': _L0_gnn_in['b_out'], 'L1_gnn_W1': _L1_gnn_in['W1'], 'L1_gnn_W2': _L1_gnn_in['W2'], 'L1_gnn_epsilons': _L1_gnn_in['epsilons'], 'L1_gnn_mlp1_w': _L1_gnn_in['mlp1_w'], 'L1_gnn_mlp1_b': _L1_gnn_in['mlp1_b'], 'L1_gnn_mlp2_w': _L1_gnn_in['mlp2_w'], 'L1_gnn_mlp2_b': _L1_gnn_in['mlp2_b'], 'L2_gnn_W': _L2_gnn_in['W'], 'L2_gnn_b': _L2_gnn_in['b'], 'L3_gnn_W_edge': _L3_gnn_in['W_edge'], 'L3_gnn_b_edge': _L3_gnn_in['b_edge'], 'L3_gnn_W1': _L3_gnn_in['W1'], 'L3_gnn_b1': _L3_gnn_in['b1'], 'L3_gnn_gamma': _L3_gnn_in['gamma'], 'L3_gnn_beta': _L3_gnn_in['beta'], 'L3_gnn_W2': _L3_gnn_in['W2'], 'L3_gnn_b2': _L3_gnn_in['b2']}

def reference(x, src, dst, edge_attr_16, L0_gnn_W_l0, L0_gnn_W_r0, L0_gnn_b_l0, L0_gnn_W_l1, L0_gnn_W_r1, L0_gnn_b_l1, L0_gnn_W_out, L0_gnn_b_out, L1_gnn_W1, L1_gnn_W2, L1_gnn_epsilons, L1_gnn_mlp1_w, L1_gnn_mlp1_b, L1_gnn_mlp2_w, L1_gnn_mlp2_b, L2_gnn_W, L2_gnn_b, L3_gnn_W_edge, L3_gnn_b_edge, L3_gnn_W1, L3_gnn_b1, L3_gnn_gamma, L3_gnn_beta, L3_gnn_W2, L3_gnn_b2):
    import jax
    import jax.numpy as jnp

    def _L0_gnn_ref(x, edge_index, W_l0, W_r0, b_l0, W_l1, W_r1, b_l1, W_out, b_out):
        import jax, jax.numpy as jnp
        import numpy as np
        N_NODES = 12500
        N_EDGES = 156250
        IN_C, HID_C, OUT_C = (64, 128, 64)

        def _sage_conv(x, src, dst, W_l, b_l, W_r):
            agg = jax.ops.segment_sum(x[src], dst, num_segments=N_NODES)
            deg = jax.ops.segment_sum(jnp.ones((src.shape[0],), x.dtype), dst, num_segments=N_NODES)
            mean = agg / jnp.maximum(deg, 1.0)[:, None]
            return mean @ W_l + b_l + x @ W_r
        src, dst = (edge_index[0], edge_index[1])
        h = jax.nn.relu(_sage_conv(x, src, dst, W_l0, b_l0, W_r0))
        h = jax.nn.relu(_sage_conv(h, src, dst, W_l1, b_l1, W_r1))
        return h @ W_out + b_out

    def _L1_gnn_ref(x, edge_index, W1, W2, epsilons, mlp1_w, mlp1_b, mlp2_w, mlp2_b):
        import jax, jax.numpy as jnp
        import numpy as np
        D = 4
        H = 16
        N = 6250
        E = 100000
        TI, TJ = np.tril_indices(D, -1)

        def _householder(params):
            A = jnp.zeros(params.shape[:-1] + (D, D), params.dtype)
            A = A.at[..., TI, TJ].set(params) + jnp.eye(D, dtype=params.dtype)
            Q, R = jnp.linalg.qr(A)
            s = jnp.sign(jnp.diagonal(R, axis1=-2, axis2=-1))
            s = jnp.where(s == 0, jnp.ones_like(s), s)
            return Q * s[..., None, :]

        def _mlp(z, w1, b1, w2, b2):
            h = jax.nn.relu(z @ w1.T + b1)
            return h @ w2.T + b2

        def _forward(x, edge_index, W1, W2, epsilons, mlp1_w, mlp1_b, mlp2_w, mlp2_b):
            n = x.shape[0]
            xr = x.reshape(n, D, H)
            xt = jnp.einsum('ndf,dk->nkf', xr, W1)
            xt = jnp.einsum('ndf,fg->ndg', xt, W2)
            loops = jnp.arange(n)
            row = jnp.concatenate([edge_index[0], loops])
            col = jnp.concatenate([edge_index[1], loops])
            deg = jax.ops.segment_sum(jnp.ones_like(row, x.dtype), row, num_segments=n)
            dis = jnp.where(deg > 0, deg ** (-0.5), jnp.zeros_like(deg))
            xf = xt.reshape(n, D * H)
            xi = xf[col]
            xj = xf[row]
            cat_ve = jnp.concatenate([xi, xj], axis=-1)
            cat_ue = jnp.concatenate([xj, xi], axis=-1)
            Fve = _householder(_mlp(cat_ve, mlp1_w, mlp1_b, mlp2_w, mlp2_b))
            Fue = _householder(_mlp(cat_ue, mlp1_w, mlp1_b, mlp2_w, mlp2_b))
            xjr = xj.reshape(-1, D, H)
            msg = jnp.einsum('eka,ekb,ebh->eah', Fve, Fue, xjr)
            msg = msg * (dis[col] * dis[row])[:, None, None]
            agg = jax.ops.segment_sum(msg.reshape(-1, D * H), col, num_segments=n)
            lap = jax.nn.elu(agg.reshape(n, D, H))
            coeff = (1.0 + jnp.tanh(epsilons))[None, :, None]
            return (coeff * xr - lap).reshape(n, D * H)
        return _forward(x, edge_index, W1, W2, epsilons, mlp1_w, mlp1_b, mlp2_w, mlp2_b)

    def _L2_gnn_ref(features, src, tgt, W, b):
        import jax, jax.numpy as jnp
        import numpy as np
        V = 12500
        E = 200000
        C_IN = 64
        C_OUT = 64
        num_v = features.shape[0]
        local = features[tgt]
        nbr = features[src]
        x = jnp.concatenate([local, nbr - local], axis=-1)
        y = jnp.einsum('ec,oc->eo', x, W) + b
        s = jax.ops.segment_sum(y, tgt, num_segments=num_v)
        cnt = jax.ops.segment_sum(jnp.ones((y.shape[0],), y.dtype), tgt, num_segments=num_v)
        cnt = cnt[:, None]
        return jnp.where(cnt > 0, s / jnp.maximum(cnt, 1.0), 0.0)

    def _L3_gnn_ref(x, edge_index, edge_attr, W_edge, b_edge, W1, b1, gamma, beta, W2, b2):
        import jax, jax.numpy as jnp
        import numpy as np
        N_NODES = 6250
        N_EDGES = 125000
        IN_SIZE = 64
        OUT_SIZE = 64
        EDGE_DIM = 16
        BN_EPS = 1e-05
        GIN_EPS = 0.0
        src = edge_index[0]
        dst = edge_index[1]
        ea = edge_attr @ W_edge.T + b_edge
        msg = jax.nn.relu(x[src] + ea)
        agg = jax.ops.segment_sum(msg, dst, num_segments=x.shape[0])
        h = (1.0 + GIN_EPS) * x + agg
        h = h @ W1.T + b1
        mean = jnp.mean(h, axis=0)
        var = jnp.var(h, axis=0)
        h = gamma * (h - mean) * jax.lax.rsqrt(var + BN_EPS) + beta
        h = jax.nn.relu(h)
        return h @ W2.T + b2
    edge_index = jnp.stack([src, dst])
    h = jnp.maximum(_layernorm(x, axis=-1), 0.0)
    x = x + _L0_gnn_ref(h, edge_index, L0_gnn_W_l0, L0_gnn_W_r0, L0_gnn_b_l0, L0_gnn_W_l1, L0_gnn_W_r1, L0_gnn_b_l1, L0_gnn_W_out, L0_gnn_b_out)
    h = jnp.maximum(_layernorm(x, axis=-1), 0.0)
    x = x + _L1_gnn_ref(h, edge_index, L1_gnn_W1, L1_gnn_W2, L1_gnn_epsilons, L1_gnn_mlp1_w, L1_gnn_mlp1_b, L1_gnn_mlp2_w, L1_gnn_mlp2_b)
    h = jnp.maximum(_layernorm(x, axis=-1), 0.0)
    x = x + _L2_gnn_ref(h, src, dst, L2_gnn_W, L2_gnn_b)
    h = jnp.maximum(_layernorm(x, axis=-1), 0.0)
    x = x + _L3_gnn_ref(h, edge_index, edge_attr_16, L3_gnn_W_edge, L3_gnn_b_edge, L3_gnn_W1, L3_gnn_b1, L3_gnn_gamma, L3_gnn_beta, L3_gnn_W2, L3_gnn_b2)
    return x

_drawn_inputs = setup_inputs


def setup_inputs(seed=0):
    import zlib

    import numpy as np

    out = dict(_drawn_inputs(seed))
    spreads = {'L0_gnn_b_l0': (0.0, 0.1),
     'L0_gnn_b_l1': (0.0, 0.1),
     'L0_gnn_b_out': (0.0, 0.1),
     'L1_gnn_epsilons': (0.0, 0.1),
     'L1_gnn_mlp1_b': (0.0, 0.8),
     'L1_gnn_mlp2_b': (0.0, 0.8),
     'L3_gnn_b_edge': (0.0, 0.439),
     'L3_gnn_b1': (0.0, 0.8),
     'L3_gnn_gamma': (1.0, 0.2),
     'L3_gnn_beta': (0.0, 0.455),
     'L3_gnn_b2': (0.0, 0.1)}
    factors = {'L2_gnn_b': 8.0}
    for name, (base, spread) in spreads.items():
        noise = np.random.default_rng([zlib.crc32(name.encode()), seed]).standard_normal(out[name].shape)
        drawn = base * np.exp(spread * noise) if base else spread * noise
        out[name] = jnp.asarray(drawn.astype(out[name].dtype))
    for name, factor in factors.items():
        out[name] = (out[name] * factor).astype(out[name].dtype)
    return out
```

```python
import concourse.bass as bass
from concourse import mybir
from contextlib import ExitStack

F32 = mybir.dt.float32
BF16 = mybir.dt.bfloat16
I32 = mybir.dt.int32
ALU = mybir.AluOpType
ACT = mybir.ActivationFunctionType
AX = mybir.AxisListType

P = 128
UT = 8
GE = UT * P
C = 64
HID = 128
D, H = 4, 16
NPAR = D * (D - 1) // 2
EDIM = 16
EPS = 1e-5

SAGE0, SAGE1, SHEAF, LINEAR, GIN = range(5)


class Chain:

    def __init__(self, eng, sem, before=0):
        self.eng, self.sem, self.before, self.i, self.per, self.n = eng, sem, before, 0, 0, 0

    def enter(self, i, per):
        self.before += self.n
        self.i, self.per, self.n = i, per, 0

    def leave(self, rounds):
        assert self.n == self.per, f"{self.n} instructions are counted in a round, not {self.per}"
        self.before += self.per * rounds
        self.i = self.per = self.n = 0

    def add(self, ins):
        ins.then_inc(self.sem, 1)
        self.n += 1

    def value(self):
        return self.i * self.per + (self.before + self.n)

    def wait(self):
        self.eng.wait_ge(self.sem, self.value())


def gnn_kernel(nc, x, src, dst, edge_attr_16, W_l0, W_r0, b_l0, W_l1, W_r1, b_l1, W_out, b_out,
               sW1, sW2, epsilons, mlp1_w, mlp1_b, mlp2_w, mlp2_b, linW, lin_b,
               W_edge, b_edge, gW1, gb1, gamma, beta, gW2, gb2, out):
    N, E = x.shape[0], src.shape[0]
    NG = 2 * -(-E // (2 * GE))
    NPAIR = NG // 2
    BLOCKS = -(-N // P)
    NNG = -(-(N + P) // GE)
    NB = NNG * UT
    NPAD = NB * P
    PAD_DST = NPAD - 1
    assert PAD_DST >= max(BLOCKS * P, N - 1 + P)
    GFULL, ETAIL = divmod(E, GE)
    BN = next(c for c in range(512, 0, -1) if N % c == 0)
    NBN = N // BN

    ctx = ExitStack()
    with ctx:
        ctx.enter_context(nc.allow_non_contiguous_dma(reason="small transposed weights"))

        def sb(name, shape, dt=F32):
            return ctx.enter_context(nc.sbuf_tensor(name, shape, dt))

        def sem(name):
            return ctx.enter_context(nc.semaphore(name))

        def dram(name, shape):
            return nc.dram_tensor(name, shape, F32, kind="Internal").ap()

        tab_h0 = dram("tab_h0", (NPAD, C))
        tab_h1 = dram("tab_h1", (NPAD, HID))
        tab_xr = dram("tab_xr", (NPAD, C))
        tab_sheaf = dram("tab_sheaf", (NPAD, C + 2 * H))
        tab_pq = dram("tab_pq", (NPAD, 2 * H))
        tab_h3 = dram("tab_h3", (NPAD, C))
        tab_h4 = dram("tab_h4", (NPAD, C))

        srcI = sb("srcI", [P, NG * UT], I32)
        dstI = sb("dstI", [P, NG * UT], I32)
        rel = sb("rel", [P, NG * UT], BF16)
        srcHi = sb("srcHi", [P, NG * UT], BF16)
        srcLo = sb("srcLo", [P, NG * UT], BF16)
        winI = sb("winI", [P, NG], I32)
        acc = sb("acc", [P, NPAD + P])
        hT = sb("hT", [P, NPAD])
        X = sb("X", [P, NB, C])
        degS = sb("degS", [P, NB])
        rdeg = sb("rdeg", [P, NB])
        ind = sb("ind", [P, NB])
        hist = sb("hist", [P, P])
        ident = sb("ident", [P, P])
        iotaB = sb("iotaB", [P, P], BF16)
        ones = sb("ones", [P, P])
        off = sb("off", [P, 1])
        flagI = sb("flagI", [P, 1], I32)

        wl0 = sb("wl0", [C, HID])
        wr0 = sb("wr0", [C, HID])
        wl1 = sb("wl1", [HID, HID])
        wr1 = sb("wr1", [HID, HID])
        wout = sb("wout", [HID, C])
        kron = sb("kron", [C, C])
        w1rep = sb("w1rep", [C, D])
        w2rep = sb("w2rep", [C, H])
        proj = sb("proj", [C, C + 2 * H])
        w2bd = sb("w2bd", [P, UT * NPAR])
        w2T = sb("w2T", [H, NPAR])
        weT = sb("weT", [EDIM, C])
        webd = sb("webd", [P, UT * C])
        linA = sb("linA", [C, C])
        linB = sb("linB", [C, C])
        gw1T = sb("gw1T", [C, C])
        gw2T = sb("gw2T", [C, C])
        brow = sb("brow", [1, 2 * HID + 3 * C + C + 2 * H + UT * NPAR])
        o = [0]

        def bias_row(n):
            o[0] += n
            return brow[0:1, o[0] - n:o[0]]

        bl0r, bl1r, boutr, linbr, gb2r = (bias_row(n) for n in (HID, HID, C, C, C))
        b1row, b2row = bias_row(C + 2 * H), bias_row(UT * NPAR)
        bedge = sb("bedge", [P, C])
        coef = sb("coef", [P, D])
        bn = sb("bn", [C, 8])
        stats = sb("stats", [C, NBN, 6])

        ixS = [sb(f"ixS{h}", [P, UT], I32) for h in range(2)]
        ixD = [sb(f"ixD{h}", [P, UT], I32) for h in range(2)]
        ringS = [sb(f"ringS{h}", [P, UT, HID]) for h in range(2)]
        ringD = [sb(f"ringD{h}", [P, UT, 2 * H]) for h in range(2)]
        attr = [sb(f"attr{h}", [P, UT * EDIM]) for h in range(2)]
        onehot = [sb(f"onehot{h}", [P, UT, P]) for h in range(2)]
        cur = [sb(f"cur{h}", [P, UT]) for h in range(2)]
        msg = [sb(f"msg{h}", [P, UT, C]) for h in range(2)]

        hpre = sb("hpre", [P, UT, 2, H])
        hreT = sb("hreT", [P, 2 * P])
        par = sb("par", [P, 2 * UT, NPAR])
        vecR = sb("vecR", [P, 2 * UT, D, D])
        vecV = sb("vecV", [P, 2 * UT, D, D])
        vecA = sb("vecA", [P, 2 * UT, D, D])
        vecB = sb("vecB", [P, 2 * UT, D, D])
        prod = sb("prod", [P, UT, D, D, D])
        sc = [sb(f"sc{k}", [P, 2 * UT, D]) for k in range(3)]
        rot = sb("rot", [P, UT, D, D])
        stA = sb("stA", [P, GE])
        stH = sb("stH", [P, GE])
        rows = onehot[1]
        xc, hrow = (onehot[0][:, k * 4:(k + 1) * 4, :].rearrange("p b (c f) -> p (b c) f", f=C) for k in range(2))
        sq = ringS[0][:, :, 0:C]
        hi1, lo1 = (stA[:, k * 512:(k + 1) * 512].bitcast(BF16).rearrange("p (t f) -> p t f", f=P) for k in range(2))
        lnS = [sb(f"lnS{k}", [P, UT]) for k in range(4)]

        psA, psB, psC, psD = (ctx.enter_context(nc.psum_tensor(f"ps{k}", [P, GE], F32)) for k in "ABCD")
        sums = [psA[:, 0:P], psA[:, 512:512 + P]]
        preT = psB[:, 0:2 * P]
        parP = psB[:, 512:512 + 2 * UT * NPAR].rearrange("p (x k) -> p x k", k=NPAR)
        edgeP = psC[:, 0:UT * C]
        histP = psD[:, 0:P]

        dstF, winF = acc[:, 0:NG * UT], acc[:, NG * UT:NG * UT + NG]

        def blocks(t, width, pitch=None):
            pitch = pitch or width
            return t[:, 0:UT * pitch].rearrange("p (b f) -> p b f", f=pitch)[:, :, 0:width]


        def pair(name):
            return [sem(f"{name}{h}") for h in range(2)]

        padded, indices_in, x_in = sem("padded"), sem("indices_in"), sem("x_in")
        cleared, weights_in, rows_spread = sem("cleared"), sem("weights_in"), sem("rows_spread")
        consts, weights_done, tanh_done = sem("consts"), sem("weights_done"), sem("tanh_done")
        dst_ready, win_summed, off_ready, off_summed = (sem(n) for n in ("dst_ready", "win_summed", "off_ready",
                                                                         "off_summed"))
        prepared, attr_tail = sem("prepared"), sem("attr_tail")
        dve_chain = sem("dve_chain")
        cur_moved = pair("cur_moved")
        sp_turns, pool_turns, pe_turns, act_turns, dve_turns = (
            sem(n) for n in ("sp_turns", "pool_turns", "pe_turns", "act_turns", "dve_turns"))
        stored = sem("stored")

        index_ready, index_dst_ready = pair("index_ready"), pair("index_dst_ready")
        gathered_early, gathered_late, gathered_dst = pair("gathered_early"), pair("gathered_late"), pair("gathered_dst")
        gathered = [gathered_early] * 3 + [gathered_late] * 2
        attr_in = pair("attr_in")
        onehot_ready, summed, added, msg_ready = pair("onehot_ready"), pair("summed"), pair("added"), pair("msg_ready")
        hist_ready, hist_summed = sem("hist_ready"), sem("hist_summed")
        hist_added, hist_T, deg_ready, deg_root = sem("hist_added"), sem("hist_T"), sem("deg_ready"), sem("deg_root")
        deg_done = sem("deg_done")

        pre_ready, preT_ready, hid_ready, par_ready = (sem(n) for n in ("pre_ready", "preT_ready", "hid_ready",
                                                                        "par_ready"))
        par_copied, norm2_ready, norm_ready = sem("par_copied"), sem("norm2_ready"), sem("norm_ready")
        attrT_ready, attrT_copied, edge_ready, pre_relu = (sem(n) for n in ("attrT_ready", "attrT_copied",
                                                                            "edge_ready", "pre_relu"))

        USES = {
            "staged": (1, 2, 3, 4, 5, 6), "mixed": (1, 2, 3, 4, 5, 6), "scaled": (1, 2),
            "hid": (1, 2), "hid_T": (1, 2), "hid_T_copied": (1, 2), "outed": (2,),
            "var": (0, 2, 3, 4), "std": (0, 2, 3, 4), "ln": (0, 2, 3, 4), "ln_T": (0, 2, 3, 4),
            "ln_T_copied": (0, 2, 3, 4), "xf_T": (2,), "xf_T_copied": (2,), "table_mm": (2,), "table_dve": (2,),
            "table_act": (2,), "loop_msg": (2,), "loop_T": (2,), "loop_T_copied": (2,),
            "exp_in": (3,), "exp_out": (3,), "biased": (4,), "bn_in": (5,), "bn_stat": (5,), "result": (6,),
        }
        ROUNDS = (NNG, NNG, NNG, NNG, NNG, NBN, NNG)
        node = {name: sem(name) for name in USES}
        xr_in = sem("xr_in")
        bn_var, bn_std, bn_done = sem("bn_var"), sem("bn_std"), sem("bn_done")
        STORES = (1, 1, 3, 1, 1)
        result_out = sem("result_out")

        def at(name, k, j):
            return j + (2 + sum(ROUNDS[u] for u in USES[name] if u < k))

        def before(name, k, j):
            return j + (1 + sum(ROUNDS[u] for u in USES[name] if u < k))

        def stores(k, j):
            return j * (16 * STORES[k]) + 16 * NNG * sum(STORES[:k])

        def gathers(k, i):
            return i * (16 * UT) + 16 * UT * NPAIR * (k % 3)

        def windows(k, i, W):
            return i * W + (1 + NPAIR * W * k)

        def held(eng, turn, *waits):
            for s, value in waits:
                eng.wait_ge(s, value)
            eng.sem_inc(turn, 1)

        def half(t, i, h):
            return t[:, bass.ds(i * (2 * UT) + h * UT, UT)]

        def by_windows(eng, run):
            eng.wait_ge(prepared, 1)
            flag = eng.value_load(flagI[0:1, 0:1], min_val=0, max_val=1)
            with eng.If(flag > 0):
                run(BLOCKS)
            with eng.Else():
                run(1)

        def over_windows(eng, W, step):
            if W == 1:
                step(0)
            else:
                with eng.Fori(0, W) as w:
                    step(w)

        nfull, ntail = divmod(N, P)
        block = ctx.enter_context(nc.Block())

        @block.sync
        def _(sp):
            for t, a, n in ((srcI, src, 1), (dstI, dst, 2)):
                sp.wait_ge(padded, n)
                v = t[:, :].rearrange("p (g u) -> p g u", u=UT)
                sp.dma_start(v[:, 0:GFULL, :], a[0:GFULL * GE].rearrange("(g p u) -> p g u", p=P, u=UT))\
                    .then_inc(indices_in, 16)
                q, r = divmod(ETAIL, UT)
                if q:
                    sp.dma_start(v[0:q, GFULL, :],
                                 a[GFULL * GE:GFULL * GE + q * UT].rearrange("(p u) -> p u", u=UT))\
                        .then_inc(indices_in, 16)
                if r:
                    sp.dma_start(v[q:q + 1, GFULL, 0:r],
                                 a[GFULL * GE + q * UT:E].rearrange("(p u) -> p u", p=1)).then_inc(indices_in, 16)
            sp.wait_ge(padded, 3)
            sp.dma_start(X[:, 0:nfull, :], x[0:nfull * P, :].rearrange("(b p) f -> p b f", p=P)).then_inc(x_in, 16)
            if ntail:
                sp.dma_start(X[0:ntail, nfull, :], x[nfull * P:N, :]).then_inc(x_in, 16)

            def same(a, parts, n):
                return bass.AP(tensor=a.tensor, offset=a.offset, ap=[[0, parts], [1, n]])

            def turned(a, rows_, c0, cols):
                return bass.AP(tensor=a.tensor, offset=a.offset + c0,
                               ap=[[1, cols], [a.shape[1], rows_], [1, 1]])

            def cells(t, a, b):
                return t[:, a:b].rearrange("p (f o) -> p f o", o=1)

            sp.wait_ge(cleared, 4)
            loads = [(wl0[:, :], W_l0), (wr0[:, :], W_r0), (wl1[:, :], W_l1), (wr1[:, :], W_r1), (wout[:, :], W_out),
                     (bl0r, same(b_l0, 1, HID)), (bl1r, same(b_l1, 1, HID)), (boutr, same(b_out, 1, C)),
                     (linbr, same(lin_b, 1, C)), (gb2r, same(gb2, 1, C)), (b1row[:, C:C + H], same(mlp1_b, 1, H)),
                     (bedge[:, :], same(b_edge, P, C)), (coef[:, :], same(epsilons, P, D)),
                     (cells(proj, C, C + H), turned(mlp1_w, H, 0, C)),
                     (cells(proj, C + H, C + 2 * H), turned(mlp1_w, H, C, C)),
                     (cells(w2T, 0, NPAR), turned(mlp2_w, NPAR, 0, H)), (cells(weT, 0, C), turned(W_edge, C, 0, EDIM)),
                     (cells(linA, 0, C), turned(linW, C, 0, C)), (cells(linB, 0, C), turned(linW, C, C, C)),
                     (cells(gw1T, 0, C), turned(gW1, C, 0, C)), (cells(gw2T, 0, C), turned(gW2, C, 0, C))]
            loads += [(bn[:, k:k + 1], a.rearrange("(p o) -> p o", o=1)) for k, a in enumerate((gb1, gamma, beta))]
            loads += [(w1rep[d * H:(d + 1) * H, :],
                       bass.AP(tensor=sW1.tensor, offset=sW1.offset + d * D, ap=[[0, H], [1, D]])) for d in range(D)]
            loads += [(w2rep[d * H:(d + 1) * H, :], sW2) for d in range(D)]
            loads += [(b2row[:, u * NPAR:(u + 1) * NPAR], same(mlp2_b, 1, NPAR)) for u in range(UT)]
            for t, a in loads:
                sp.dma_start(t, a).then_inc(weights_in, 16)
            sp.wait_ge(weights_in, 16 * len(loads))
            for u in range(UT):
                sp.dma_start(w2bd[u * H:(u + 1) * H, u * NPAR:(u + 1) * NPAR], w2T[:, :]).then_inc(rows_spread, 16)
                sp.dma_start(webd[u * EDIM:(u + 1) * EDIM, u * C:(u + 1) * C], weT[:, :]).then_inc(rows_spread, 16)

            def table(t, j):
                return t[bass.ds(j * GE, GE), :].rearrange("(b p) f -> p b f", p=P)

            def indices(k, i, h, first=False):
                if not first:
                    held(sp, sp_turns, (gathered[k][h], gathers(k, i)))
                elif k > 0:
                    held(sp, sp_turns, (gathered[k - 1][h], gathers(k - 1, NPAIR)))
                sp.dma_start(ixS[h][:, :], half(srcI, i, h)).then_inc(index_ready[h], 16)
                if k == SHEAF:
                    if not first:
                        held(sp, sp_turns, (gathered_dst[h], gathers(0, i)))
                    sp.dma_start(ixD[h][:, :], half(dstI, i, h)).then_inc(index_dst_ready[h], 16)

            def index_pass(k):
                for h in range(2):
                    indices(k, 0, h, first=True)
                with sp.Fori(1, NPAIR) as i:
                    for h in range(2):
                        indices(k, i, h)

            def run(W):
                with sp.Fori(0, NNG) as j:
                    held(sp, sp_turns, (node["ln"], at("ln", 0, j)))
                    sp.dma_start(table(tab_h0, j), hrow[:, :, :]).then_inc(stored, 16)
                index_pass(SAGE0)
                with sp.Fori(0, NNG) as j:
                    held(sp, sp_turns, (node["hid"], at("hid", 1, j)))
                    sp.dma_start(table(tab_h1, j), rows[:, :, :]).then_inc(stored, 16)
                index_pass(SAGE1)
                with sp.Fori(0, NNG) as j:
                    held(sp, sp_turns, (node["ln"], at("ln", 2, j)))
                    sp.dma_start(table(tab_xr, j), hrow[:, :, :]).then_inc(stored, 16)
                    held(sp, sp_turns, (node["table_dve"], at("table_dve", 2, j)))
                    held(sp, sp_turns, (node["table_act"], at("table_act", 2, j)))
                    sp.dma_start(table(tab_sheaf, j), rows[:, :, 0:C + 2 * H]).then_inc(stored, 16)
                    sp.dma_start(table(tab_pq, j), rows[:, :, C:C + 2 * H]).then_inc(stored, 16)
                index_pass(SHEAF)
                with sp.Fori(0, NNG) as j:
                    held(sp, sp_turns, (stored, stores(3, 0)))
                    held(sp, sp_turns, (node["ln"], before("ln", 3, j)))
                    held(sp, sp_turns, (node["staged"], at("staged", 3, j)))
                    sp.dma_start(rows[:, :, 0:C], table(tab_xr, j)).then_inc(xr_in, 16)
                    held(sp, sp_turns, (node["ln"], at("ln", 3, j)))
                    sp.dma_start(table(tab_h3, j), hrow[:, :, :]).then_inc(stored, 16)
                index_pass(LINEAR)
                with sp.Fori(0, NNG) as j:
                    held(sp, sp_turns, (node["biased"], at("biased", 4, j)))
                    sp.dma_start(table(tab_h4, j), rows[:, :, 0:C]).then_inc(stored, 16)

                for h in range(2):
                    indices(GIN, 0, h, first=True)
                with sp.Fori(0, NPAIR - 1) as i:
                    for h in range(2):
                        held(sp, sp_turns, (attrT_ready, i * 2 + (h + 1)))
                        sp.dma_start(attr[h][:, :], edge_attr_16[bass.ds(i * (2 * GE) + h * GE, GE), :]
                                     .rearrange("(p u) f -> p (u f)", p=P)).then_inc(attr_in[h], 16)
                    for h in range(2):
                        indices(GIN, i + 1, h)
                for h in range(2):
                    g = NG - 2 + h
                    held(sp, sp_turns, (attrT_ready, g + 1))
                    q, r = divmod(max(0, min(GE, E - g * GE)), UT)
                    if r:
                        sp.dma_start(attr[h][q:q + 1, 0:r * EDIM],
                                     edge_attr_16[g * GE + q * UT:E, :].rearrange("(p u) f -> p (u f)", p=1))\
                            .then_inc(attr_tail, 16)
                        held(sp, sp_turns, (attr_tail, 16))
                    if q:
                        sp.dma_start(attr[h][0:q, :],
                                     edge_attr_16[g * GE:g * GE + q * UT, :].rearrange("(p u) f -> p (u f)", p=q))\
                            .then_inc(attr_in[h], 16)
                    else:
                        sp.sem_inc(attr_in[h], 16)

                with sp.Fori(0, NNG - 1) as j:
                    held(sp, sp_turns, (node["result"], at("result", 6, j)))
                    sp.dma_start(out[bass.ds(j * GE, GE), :].rearrange("(b p) f -> p b f", p=P),
                                 X[:, bass.ds(j * UT, UT), :]).then_inc(result_out, 16)
                held(sp, sp_turns, (node["result"], at("result", 6, NNG - 1)))
                b0 = (NNG - 1) * UT
                if nfull > b0:
                    sp.dma_start(out[b0 * P:nfull * P, :].rearrange("(b p) f -> p b f", p=P),
                                 X[:, b0:nfull, :]).then_inc(result_out, 16)
                if ntail:
                    sp.dma_start(out[nfull * P:N, :], X[0:ntail, nfull, :]).then_inc(result_out, 16)
                held(sp, sp_turns, (result_out, 16 * (NNG - 1 + (nfull > b0) + (ntail > 0))))
                held(sp, sp_turns, (stored, stores(4, NNG)))

            by_windows(sp, run)

        @block.gpsimd
        def _(pool):
            nc.gpsimd.memset(ident[:, :], 0.0).then_inc(pool_turns, 1)
            nc.gpsimd.memset(onehot[0][:, 0, :], 0.0).then_inc(pool_turns, 1)
            pool.wait_ge(pool_turns, 2)
            nc.gpsimd.affine_select(out=ident[:, :], in_=ident[:, :], compare_op=ALU.not_equal, fill=1.0, base=0,
                                    pattern=[[-1, P]], channel_multiplier=1).then_inc(consts, 1)
            nc.gpsimd.affine_select(out=onehot[0][:, 0, :], in_=onehot[0][:, 0, :], compare_op=ALU.not_equal, fill=1.0, base=0,
                                    pattern=[[0, P]], channel_multiplier=1).then_inc(consts, 1)
            nc.gpsimd.iota(iotaB[:, :], pattern=[[1, P]], base=0, channel_multiplier=0,
                           allow_small_or_imprecise_dtypes=True).then_inc(consts, 1)

            def gather(table, slot, index, done):
                pool.indirect_dma_start(slot, None, table[:, :], bass.IndirectOffsetOnAxis(ap=index, axis=0))\
                    .then_inc(done, 16)

            def run(W):
                tables = {SAGE0: (tab_h0, C), SAGE1: (tab_h1, HID), SHEAF: (tab_sheaf, C + 2 * H),
                          LINEAR: (tab_h3, C), GIN: (tab_h4, C)}
                for k, (tab, width) in tables.items():
                    held(pool, pool_turns, (stored, stores(k, NNG)))
                    with pool.Fori(0, NPAIR) as i:
                        for h in range(2):
                            pool.wait_ge(index_ready[h], i * 16 + 16 * (1 + NPAIR * k))
                            if k == SHEAF:
                                pool.wait_ge(index_dst_ready[h], i * 16 + 16)
                            held(pool, pool_turns, (summed[h], windows(k, i, W)))
                            for u in range(UT):
                                gather(tab, ringS[h][:, u, 0:width], ixS[h][:, u:u + 1], gathered[k][h])
                                if k == SHEAF:
                                    gather(tab_pq, ringD[h][:, u, :], ixD[h][:, u:u + 1], gathered_dst[h])

            by_windows(pool, run)

        @block.scalar
        def _(act):
            def copy(out_, in_):
                return nc.scalar.activation(out_, in_, ACT.Copy)

            act.wait_ge(rows_spread, 32 * UT)
            nc.scalar.activation(coef[:, :], coef[:, :], ACT.Tanh).then_inc(tanh_done, 1)

            def sheaf(n):
                act.wait_ge(preT_ready, n)
                nc.scalar.activation(hreT[:, :], preT, ACT.Relu).then_inc(hid_ready, 1)
                act.wait_ge(par_ready, n)
                copy(vecR[:, :, 0, 1:3], parP[:, :, 0:2])
                copy(vecR[:, :, 0, 3], parP[:, :, 3])
                copy(vecR[:, :, 1, 2:4], parP[:, :, 2:5:2])
                copy(par[:, :, :], parP).then_inc(par_copied, 1)
                act.wait_ge(norm2_ready, n)
                nc.scalar.activation(sc[2][:, :, :], sc[0][:, :, :], ACT.Sqrt).then_inc(norm_ready, 1)

            def run(W):
                def std(k, j):
                    act.wait_ge(node["var"], at("var", k, j))
                    nc.scalar.activation(lnS[2][:, :], lnS[1][:, :], ACT.Sqrt).then_inc(node["std"], 1)

                def put(k, j, ready, dest, source, done):
                    held(act, act_turns, (node[ready], at(ready, k, j)))
                    copy(dest, source).then_inc(node[done], 1)

                def stage(k, j, agg, own):
                    cols = bass.ds(j * GE, GE)
                    held(act, act_turns, (added[0], windows(k, 0, W)), (added[1], windows(k, 0, W)),
                         (node["mixed"], before("mixed", k, j)))
                    if own:
                        copy(stH[0:own, :], hT[0:own, cols])
                    copy(stA[0:agg, :], acc[0:agg, cols]).then_inc(node["staged"], 1)

                def edges(k):
                    with act.Fori(0, NPAIR) as i:
                        for h in range(2):
                            n = i * 2 + (h + 1)
                            if k == SHEAF:
                                sheaf(n + NNG)
                            if k == GIN:
                                act.wait_ge(attrT_ready, n + 2)
                                copy(hreT[:, 0:P], psB[:, 0:P]).then_inc(attrT_copied, 1)
                                act.wait_ge(summed[h], windows(k, i, W))
                                act.wait_ge(pre_relu, n)
                                nc.scalar.activation(msg[h][:, :, :], blocks(stH, C), ACT.Relu)\
                                    .then_inc(msg_ready[h], 1)

                with act.Fori(0, NNG) as j:
                    std(0, j)
                    put(0, j, "ln_T", hT[0:C, bass.ds(j * GE, GE)], psC[0:C, :], "ln_T_copied")

                act.wait_ge(deg_ready, 1)
                nc.scalar.activation(degS[:, :], degS[:, :], ACT.Sqrt).then_inc(deg_root, 1)
                with act.Fori(0, NNG) as j:
                    stage(1, j, C + 1, C)
                    act.wait_ge(node["scaled"], at("scaled", 1, j))
                    nc.scalar.activation(rows[:, :, :], rows[:, :, :], ACT.Relu).then_inc(node["hid"], 1)
                    put(1, j, "hid_T", hT[:, bass.ds(j * GE, GE)], psC[:, :], "hid_T_copied")

                with act.Fori(0, NNG) as j:
                    stage(2, j, HID, HID)
                    act.wait_ge(node["scaled"], at("scaled", 2, j))
                    nc.scalar.activation(rows[:, :, :], rows[:, :, :], ACT.Relu).then_inc(node["hid"], 1)
                    put(2, j, "hid_T", stA[:, :], psC[:, :], "hid_T_copied")
                    std(2, j)
                    put(2, j, "ln_T", stA[0:C, :], psC[0:C, :], "ln_T_copied")
                    put(2, j, "xf_T", stH[0:C, :], psB[0:C, :], "xf_T_copied")
                    put(2, j, "table_mm", rows[:, :, C:C + 2 * H],
                        psA[:, :].rearrange("p (b f) -> p b f", f=P)[:, :, C:C + 2 * H], "table_act")
                    sheaf(j + 1)
                    put(2, j, "loop_T", acc[0:C, bass.ds(j * GE, GE)], psC[0:C, :], "loop_T_copied")

                edges(SHEAF)
                with act.Fori(0, NNG) as j:
                    stage(3, j, C, 0)
                    act.wait_ge(node["exp_in"], at("exp_in", 3, j))
                    nc.scalar.activation(rows[:, :, C:2 * C], rows[:, :, C:2 * C], ACT.Exp).then_inc(node["exp_out"], 1)
                    std(3, j)
                    put(3, j, "ln_T", hT[0:C, bass.ds(j * GE, GE)], psC[0:C, :], "ln_T_copied")

                with act.Fori(0, NNG) as j:
                    stage(4, j, C, C)
                    std(4, j)
                    put(4, j, "ln_T", acc[0:C, bass.ds(j * GE, GE)], psC[0:C, :], "ln_T_copied")

                edges(GIN)
                with act.Fori(0, NBN) as m:
                    held(act, act_turns, (added[0], windows(5, 0, W)), (added[1], windows(5, 0, W)))
                    copy(stA[0:C, 0:BN], acc[0:C, bass.ds(m * BN, BN)]).then_inc(node["staged"], 1)
                    held(act, act_turns, (node["mixed"], at("mixed", 5, m)))
                    nc.scalar.activation(hT[0:C, bass.ds(m * BN, BN)], psA[0:C, 0:BN], ACT.Identity,
                                         bias=bn[:, 0:1]).then_inc(node["bn_in"], 1)
                act.wait_ge(bn_var, 1)
                nc.scalar.activation(bn[:, 5:6], bn[:, 4:5], ACT.Sqrt).then_inc(bn_std, 1)

                with act.Fori(0, NNG) as j:
                    held(act, act_turns, (bn_done, 1), (node["mixed"], before("mixed", 6, j)),
                         (node["bn_in"], at("bn_in", 5, NBN - 1)))
                    nc.scalar.activation(stA[0:C, :], hT[0:C, bass.ds(j * GE, GE)], ACT.Relu, bias=bn[:, 7:8],
                                         scale=bn[:, 6:7]).then_inc(node["staged"], 1)

            by_windows(act, run)

        @block.tensor
        def _(pe):
            def mm(out_, lhsT, rhs, start=True, stop=True):
                return nc.tensor.matmul(out_, lhsT, rhs, start=start, stop=stop)

            def biased(out_, pairs, bias):
                for n, (lhsT, rhs) in enumerate(pairs):
                    mm(out_, lhsT, rhs, start=(n == 0), stop=False)
                return mm(out_, ones[0:1, :], bias, start=False, stop=True)

            def turn(out_, in_):
                return nc.tensor.transpose(out_, in_, ident[0:in_.shape[0], 0:in_.shape[0]])

            def cut(t, b, parts=P, pitch=P):
                return t[0:parts, b * pitch:(b + 1) * pitch]

            pe.wait_ge(consts, 3)
            pe.wait_ge(dst_ready, 1)
            mm(psA[:, 0:NG], onehot[0][:, 0, :], dstF.rearrange("p (g u) -> p g u", u=UT)[:, :, 0]).then_inc(win_summed, 1)
            pe.wait_ge(off_ready, 1)
            mm(psA[:, 512:513], ones[:, :], off[:, :]).then_inc(off_summed, 1)
            pe.wait_ge(rows_spread, 32 * UT)
            pe.wait_ge(weights_done, 1)

            def sheaf(n):
                held(pe, pe_turns, (pre_ready, n))
                for t in range(2):
                    last = turn(preT[:, t * P:(t + 1) * P],
                                hpre[:, t * 4:(t + 1) * 4, :, :].rearrange("p t s k -> p (t s k)"))
                last.then_inc(preT_ready, 1)
                held(pe, pe_turns, (hid_ready, n))
                wide = UT * NPAR
                for t in range(2):
                    last = biased(psB[:, 512 + t * wide:512 + (t + 1) * wide],
                                  [(hreT[:, t * P:(t + 1) * P], w2bd[:, :])], b2row)
                last.then_inc(par_ready, 1)

            def run(W):
                def node_T(k, j, ready, source, width, done):
                    held(pe, pe_turns, (node[ready], at(ready, k, j)))
                    for b in range(UT):
                        last = turn(psC[0:width, b * P:(b + 1) * P], source[:, b, :])
                    last.then_inc(node[done], 1)

                def edges(k):
                    with pe.Fori(0, NPAIR) as i:
                        for h in range(2):
                            n = i * 2 + (h + 1)
                            if k == SHEAF:
                                sheaf(n + NNG)
                            if k == GIN:
                                held(pe, pe_turns, (attr_in[h], i * 16 + 16))
                                turn(psB[:, 0:P], attr[h][:, :]).then_inc(attrT_ready, 1)
                                held(pe, pe_turns, (attrT_copied, n))
                                mm(edgeP, hreT[:, 0:P], webd[:, :]).then_inc(edge_ready, 1)
                            if k == SAGE0:
                                held(pe, pe_turns, (hist_ready, n))
                                for u in range(UT):
                                    last = mm(histP, hi1[:, u, :], lo1[:, u, :], start=(u == 0), stop=(u == UT - 1))
                                last.then_inc(hist_summed, 1)
                            if k in (SHEAF, GIN):
                                held(pe, pe_turns, (msg_ready[h], i + (1 + (NPAIR if k == GIN else 0))))
                                lhs, M = msg[h], C
                            else:
                                held(pe, pe_turns, (gathered[k][h], gathers(k, i + 1)))
                                M = {SAGE0: C + 1, SAGE1: HID, LINEAR: C}[k]
                                lhs = ringS[h]

                            def window(w):
                                done = i * W + w + (1 + NPAIR * W * k)
                                held(pe, pe_turns, (onehot_ready[h], done), (added[h], done))
                                for u in range(UT):
                                    last = mm(sums[h][0:M, :], lhs[:, u, 0:M], onehot[h][:, u, :], start=(u == 0),
                                              stop=(u == UT - 1))
                                last.then_inc(summed[h], 1)

                            over_windows(pe, W, window)

                with pe.Fori(0, NNG) as j:
                    node_T(0, j, "ln", hrow, C, "ln_T")
                edges(SAGE0)

                pe.wait_ge(node["ln_T_copied"], at("ln_T_copied", 0, NNG - 1))
                pe.wait_ge(hist_added, 1)
                turn(psC[:, 0:P], hist[:, :]).then_inc(hist_T, 1)
                pe.wait_ge(deg_ready, 1)
                with pe.Fori(0, NNG) as j:
                    held(pe, pe_turns, (node["staged"], at("staged", 1, j)))
                    for b in range(UT):
                        mm(cut(psA, b), cut(stA, b, C), wl0[:, :])
                        biased(cut(psB, b), [(cut(stH, b, C), wr0[:, :])], bl0r)
                        last = mm(psD[:, b:b + 1], stA[C:C + 1, b * P:(b + 1) * P], ones[C:C + 1, 0:1])
                    last.then_inc(node["mixed"], 1)
                    node_T(1, j, "hid", rows, HID, "hid_T")
                edges(SAGE1)

                with pe.Fori(0, NNG) as j:
                    held(pe, pe_turns, (node["staged"], at("staged", 2, j)))
                    for b in range(UT):
                        mm(cut(psA, b), cut(stA, b), wl1[:, :])
                        last = biased(cut(psB, b), [(cut(stH, b), wr1[:, :])], bl1r)
                    last.then_inc(node["mixed"], 1)
                    node_T(2, j, "hid", rows, HID, "hid_T")
                    held(pe, pe_turns, (node["hid_T_copied"], at("hid_T_copied", 2, j)))
                    for b in range(UT):
                        last = biased(cut(psD, b, P, C), [(cut(stA, b), wout[:, :])], boutr)
                    last.then_inc(node["outed"], 1)
                    node_T(2, j, "ln", hrow, C, "ln_T")
                    held(pe, pe_turns, (node["ln_T_copied"], at("ln_T_copied", 2, j)))
                    for b in range(2):
                        last = mm(psB[0:C, b * 512:(b + 1) * 512], kron[:, :], stA[0:C, b * 512:(b + 1) * 512])
                    last.then_inc(node["xf_T"], 1)
                    held(pe, pe_turns, (node["xf_T_copied"], at("xf_T_copied", 2, j)))
                    for b in range(UT):
                        last = biased(psA[:, b * P:b * P + C + 2 * H], [(cut(stH, b, C), proj[:, :])], b1row)
                    last.then_inc(node["table_mm"], 1)
                    sheaf(j + 1)
                    node_T(2, j, "loop_msg", msg[0], C, "loop_T")
                edges(SHEAF)

                with pe.Fori(0, NNG) as j:
                    held(pe, pe_turns, (node["staged"], at("staged", 3, j)))
                    for b in range(UT):
                        last = turn(cut(psA, b, P, C), cut(stA, b, C))
                    last.then_inc(node["mixed"], 1)
                    node_T(3, j, "ln", hrow, C, "ln_T")
                edges(LINEAR)

                with pe.Fori(0, NNG) as j:
                    held(pe, pe_turns, (node["staged"], at("staged", 4, j)))
                    for b in range(UT):
                        mm(cut(psA, b, P, C), cut(stA, b, C), linB[:, :])
                        last = biased(cut(psB, b, P, C), [(cut(stH, b, C), linA[:, :])], linbr)
                    last.then_inc(node["mixed"], 1)
                    node_T(4, j, "ln", hrow, C, "ln_T")
                edges(GIN)

                with pe.Fori(0, NBN) as m:
                    held(pe, pe_turns, (node["staged"], at("staged", 5, m)))
                    mm(psA[0:C, 0:BN], gw1T[:, :], stA[0:C, 0:BN]).then_inc(node["mixed"], 1)
                with pe.Fori(0, NNG) as j:
                    held(pe, pe_turns, (node["staged"], at("staged", 6, j)), (node["result"], before("result", 6, j)))
                    for b in range(UT):
                        last = biased(cut(psB, b, P, C), [(cut(stA, b, C), gw2T[:, :])], gb2r)
                    last.then_inc(node["mixed"], 1)

            by_windows(pe, run)

        @block.vector
        def _(dve):
            ch = Chain(dve, dve_chain)
            v = nc.vector

            def tt(out_, a, b, op):
                return v.tensor_tensor(out_, a, b, op)

            def along(a, axis, n):
                a = a.unsqueeze(axis)
                shape = list(a.shape)
                shape[axis] = n
                return a.to_broadcast(shape)

            g0 = GFULL * UT
            v.memset(srcI[:, g0:NG * UT], 0).then_inc(padded, 1)
            v.memset(dstI[:, g0:NG * UT], PAD_DST).then_inc(padded, 1)
            v.memset(X[:, nfull:NB, :], 0.0).then_inc(padded, 1)
            v.memset(brow[:, :], 0.0).then_inc(cleared, 1)
            v.memset(w2bd[:, :], 0.0).then_inc(cleared, 1)
            v.memset(webd[:, :], 0.0).then_inc(cleared, 1)
            v.memset(ones[:, :], 1.0)
            v.memset(vecR[:, :, :, :], 0.0)
            for h in range(2):
                v.memset(ringS[h][:, :, :], 1.0)
                v.memset(attr[h][:, :], 0.0)
            ch.add(v.memset(hist[:, :], 0.0))
            dve.wait_ge(consts, 3)
            ch.wait()
            for k in range(2):
                v.memset(vecR[:, :, k, k:k + 1], 1.0)
                v.memset(vecR[:, :, 3 - k, 3 - k:4 - k], 1.0)
            v.tensor_copy(proj[:, 0:C], ident[0:C, 0:C]).then_inc(cleared, 1)
            for s in [*node.values(), *summed, *added]:
                dve.sem_inc(s, 1)
            dve.sem_inc(attrT_ready, 2)
            dve.sem_inc(hist_summed, 1)

            rem, offs, real = (hT[:, k * NG * UT:(k + 1) * NG * UT] for k in range(3))

            def by_group(a):
                return a.rearrange("p (g u) -> p g u", u=UT)

            dve.wait_ge(indices_in, 16 * 2 * (1 + bool(ETAIL // UT) + bool(ETAIL % UT)))
            v.tensor_copy(dstF, dstI[:, :]).then_inc(dst_ready, 1)
            dve.wait_ge(dst_ready, 1)
            ch.add(v.tensor_scalar(real, dstF, float(N), None, ALU.is_lt))
            dve.wait_ge(win_summed, 1)
            ch.add(v.tensor_scalar(winF, psA[:, 0:NG], float(N - 1), None, ALU.min))
            ch.wait()
            v.tensor_copy(winI[:, :], winF)
            ch.add(tt(by_group(rem), by_group(dstF), along(winF, 2, UT), ALU.subtract))
            ch.wait()
            v.tensor_copy(rel[:, :], rem)
            ch.add(v.tensor_scalar(offs, rem, float(P - 1), None, ALU.is_gt))
            ch.wait()
            ch.add(tt(offs, offs, real, ALU.mult))
            ch.add(v.tensor_scalar(rem, rem, 0.0, None, ALU.is_lt))
            ch.wait()
            ch.add(tt(offs, offs, rem, ALU.add))
            ch.wait()
            v.reduce_sum(off[:, :], offs, AX.X).then_inc(off_ready, 1)
            scratch = hT[:, 3 * NG * UT:5 * NG * UT].bitcast(I32)
            v.tensor_single_scalar(scratch[:, 0:NG * UT], srcI[:, :], 7, ALU.logical_shift_right)
            ch.add(v.tensor_single_scalar(scratch[:, NG * UT:2 * NG * UT], srcI[:, :], P - 1, ALU.bitwise_and))
            ch.wait()
            v.tensor_copy(srcHi[:, :], scratch[:, 0:NG * UT])
            ch.add(v.tensor_copy(srcLo[:, :], scratch[:, NG * UT:2 * NG * UT]))
            dve.wait_ge(rows_spread, 32 * UT)
            tt(linA[:, :], linA[:, :], linB[:, :], ALU.subtract)
            for k in range(D):
                v.tensor_scalar(kron[:, k * H:(k + 1) * H], w2rep[:, :], w1rep[:, k:k + 1], None, ALU.mult)
            dve.wait_ge(tanh_done, 1)
            v.tensor_scalar(coef[:, :], coef[:, :], 1.0, None, ALU.add).then_inc(weights_done, 1)
            ch.wait()
            ch.add(v.memset(hT[:, :], 0.0))
            ch.add(v.memset(acc[:, :], 0.0))
            dve.wait_ge(off_summed, 1)
            v.tensor_scalar(flagI[:, :], psA[:, 512:513], 1.0, None, ALU.min).then_inc(prepared, 1)
            dve.wait_ge(x_in, 16 * (1 + (ntail > 0)))
            dve.wait_ge(weights_done, 1)

            def sheaf(n, gj, gi, out_, done):
                tt(hpre[:, :, 0, :], gi[:, :, 0:H], gj[:, :, C + H:C + 2 * H], ALU.add)
                tt(hpre[:, :, 1, :], gi[:, :, H:2 * H], gj[:, :, C:C + H], ALU.add).then_inc(pre_ready, 1)
                dve.wait_ge(par_copied, n)
                tt(sc[0][:, :, 0:2], par[:, :, 1:3], along(par[:, :, 5], 2, 2), ALU.mult)
                tt(sc[0][:, :, 2], par[:, :, 2], par[:, :, 0], ALU.mult)
                v.tensor_scalar(vecR[:, :, 3, 2], par[:, :, 5], -1.0, None, ALU.mult)
                ch.add(v.tensor_scalar(vecR[:, :, 2, 1], par[:, :, 2], -1.0, None, ALU.mult))
                ch.wait()
                tt(vecR[:, :, 2, 0], sc[0][:, :, 2], par[:, :, 1], ALU.subtract)
                ch.add(tt(vecR[:, :, 3, 1], sc[0][:, :, 1], par[:, :, 4], ALU.subtract))
                ch.wait()
                ch.add(tt(sc[1][:, :, 0], vecR[:, :, 3, 1], par[:, :, 0], ALU.mult))
                ch.wait()
                ch.add(tt(sc[1][:, :, 1], sc[0][:, :, 0], sc[1][:, :, 0], ALU.subtract))
                ch.wait()
                ch.add(tt(vecR[:, :, 3, 0], sc[1][:, :, 1], par[:, :, 3], ALU.subtract))
                ch.wait()
                base, vec = vecR[:, :, 0:4:3, :], vecR[:, :, 1:3, :]
                tt(vecA[:, :, 0:2, :], base, base, ALU.mult)
                ch.add(tt(vecA[:, :, 2:4, :], base, vec, ALU.mult))
                v.tensor_copy(vecV[:, :, 0:4:3, :], base)
                ch.wait()
                ch.add(v.reduce_sum(sc[0][:, :, :].rearrange("p x k -> p (x k)"),
                                    vecA[:, :, :, :].rearrange("p x v k -> p (x v) k"), AX.X))
                ch.wait()
                tt(vecB[:, :, 0:2, :], vec, along(sc[0][:, :, 0:2], 3, D), ALU.mult)
                ch.add(tt(vecB[:, :, 2:4, :], base, along(sc[0][:, :, 2:4], 3, D), ALU.mult))
                ch.wait()
                ch.add(tt(vecV[:, :, 1:3, :], vecB[:, :, 0:2, :], vecB[:, :, 2:4, :], ALU.subtract))
                ch.wait()
                ch.add(tt(vecA[:, :, :, :].rearrange("p x v k -> p (x v k)"),
                          vecV[:, :, :, :].rearrange("p x v k -> p (x v k)"),
                          vecV[:, :, :, :].rearrange("p x v k -> p (x v k)"), ALU.mult))
                ch.wait()
                v.reduce_sum(sc[0][:, :, :].rearrange("p x k -> p (x k)"),
                             vecA[:, :, :, :].rearrange("p x v k -> p (x v) k"), AX.X).then_inc(norm2_ready, 1)
                dve.wait_ge(norm_ready, n)
                flat = sc[1][:, :, :].rearrange("p x k -> p (x k)")
                ch.add(v.reciprocal(flat, sc[2][:, :, :].rearrange("p x k -> p (x k)")))
                ch.wait()
                q = vecV[:, :, :, :].rearrange("p x v k -> p (x v) k")
                ch.add(tt(q, q, along(flat, 2, D), ALU.mult))
                ch.wait()
                sides = vecV[:, :, :, :].rearrange("p (t s) v k -> p t s v k", s=2)
                for a in range(D):
                    last = tt(prod[:, :, a, :, :], along(sides[:, :, 0, a, :], 2, D), sides[:, :, 1, :, :], ALU.mult)
                ch.add(last)
                ch.wait()
                ch.add(v.reduce_sum(rot[:, :, :, :].rearrange("p t a b -> p (t a b)"),
                                    prod[:, :, :, :, :].rearrange("p t a b k -> p (t a b) k"), AX.X))
                ch.wait()
                parts = [t[:, c:c + UT * C].rearrange("p (t a g) -> p t a g", a=D, g=H)
                         for t, c in ((stA, 0), (stA, UT * C), (stH, 0), (stH, UT * C))]
                for b in range(D):
                    last = tt(parts[b], along(rot[:, :, :, b], 3, H), along(gj[:, :, b * H:(b + 1) * H], 2, D),
                              ALU.mult)
                ch.add(last)
                ch.wait()
                ch.add(tt(stA[:, :], stA[:, :], stH[:, :], ALU.add))
                ch.wait()
                tt(out_.rearrange("p t f -> p (t f)"), stA[:, 0:UT * C], stA[:, UT * C:2 * UT * C], ALU.add)\
                    .then_inc(done, 1)

            SHEAF_CHAIN = 16
            start = ch.n

            def run(W):
                nonlocal ch
                ch = Chain(dve, dve_chain, start)

                def xs(j):
                    return X[:, bass.ds(j * UT, UT), :]

                def norm(k, j):
                    held(dve, dve_turns, (dve_chain, ch.value()))
                    ch.add(v.reduce_sum(lnS[0][:, :], xs(j), AX.X))
                    ch.wait()
                    ch.add(v.tensor_scalar(lnS[0][:, :], lnS[0][:, :], 1.0 / C, None, ALU.mult))
                    ch.wait()
                    ch.add(tt(xc[:, :, :], xs(j), along(lnS[0][:, :], 2, C), ALU.subtract))
                    ch.wait()
                    ch.add(tt(sq[:, :, :], xc[:, :, :], xc[:, :, :], ALU.mult))
                    ch.wait()
                    ch.add(v.reduce_sum(lnS[3][:, :], sq[:, :, :], AX.X))
                    ch.wait()
                    v.tensor_scalar(lnS[1][:, :], lnS[3][:, :], 1.0 / C, EPS, ALU.mult, ALU.add)\
                        .then_inc(node["var"], 1)
                    dve.wait_ge(node["std"], at("std", k, j))
                    ch.add(v.reciprocal(lnS[3][:, :], lnS[2][:, :]))
                    dve.wait_ge(stored, {0: stores(0, j), 2: stores(2, j), 3: stores(3, j), 4: stores(4, j)}[k])
                    dve.wait_ge(node["ln_T"], before("ln_T", k, j))
                    ch.wait()
                    v.scalar_tensor_tensor(out=hrow[:, :, :], in0=xc[:, :, :], scalar=0.0,
                                           in1=along(lnS[3][:, :], 2, C), op0=ALU.max, op1=ALU.mult)\
                        .then_inc(node["ln"], 1)

                NORM_CHAIN = 6

                def edges(k):
                    dve.wait_ge(stored, stores(k, NNG))
                    name = {SAGE0: "ln_T", SAGE1: "hid_T", SHEAF: "loop_T"}.get(k, "ln_T")
                    dve.wait_ge(node[name], at(name, k, NNG - 1))
                    per = {SHEAF: 2 * SHEAF_CHAIN, GIN: 0}.get(k, 0)
                    with dve.Fori(0, NPAIR) as i:
                        ch.enter(i, per)
                        for h in range(2):
                            n = i * 2 + (h + 1)
                            first = dve.value_load(winI[0:1, bass.ds(i * 2 + h, 1)], min_val=0, max_val=N - 1)\
                                if W == 1 else None
                            if k == SHEAF:
                                dve.wait_ge(gathered[k][h], gathers(k, i + 1))
                                dve.wait_ge(gathered_dst[h], gathers(0, i + 1))
                                dve.wait_ge(summed[h], windows(k, i, W))
                                sheaf(n + NNG, ringS[h], ringD[h], msg[h][:, :, :], msg_ready[h])
                            if k == GIN:
                                dve.wait_ge(gathered[k][h], gathers(k, i + 1))
                                if h:
                                    dve.wait_ge(msg_ready[0], i + (1 + NPAIR))
                                else:
                                    dve.wait_ge(msg_ready[1], i + NPAIR)
                                dve.wait_ge(edge_ready, n)
                                tt(blocks(stH, C), ringS[h][:, :, 0:C], edgeP.rearrange("p (t f) -> p t f", f=C),
                                   ALU.add).then_inc(pre_relu, 1)
                            if k == SAGE0:
                                dve.wait_ge(hist_summed, n)
                                tt(hi1[:, :, :], along(iotaB[:, :], 1, UT), along(half(srcHi, i, h), 2, P),
                                   ALU.is_equal)
                                tt(lo1[:, :, :], along(iotaB[:, :], 1, UT), along(half(srcLo, i, h), 2, P),
                                   ALU.is_equal).then_inc(hist_ready, 1)
                                dve.wait_ge(hist_summed, n + 1)
                                tt(hist[:, :], hist[:, :], histP, ALU.add)
                            if W > 1:
                                held(dve, dve_turns, (summed[h], windows(k, i, W)))
                                v.tensor_copy(cur[h][:, :], half(dstI, i, h)).then_inc(cur_moved[h], 1)

                            M = {SAGE0: C + 1, SAGE1: HID}.get(k, C)

                            def window(w):
                                done = i * W + w + (1 + NPAIR * W * k)
                                if W == 1:
                                    dve.wait_ge(summed[h], done)
                                    tt(onehot[h][:, :, :], along(iotaB[:, :], 1, UT), along(half(rel, i, h), 2, P),
                                       ALU.is_equal).then_inc(onehot_ready[h], 1)
                                    begin = first
                                else:
                                    dve.wait_ge(summed[h], done)
                                    dve.wait_ge(cur_moved[h], i * (W + 1) + w + (1 + NPAIR * (W + 1) * k))
                                    tt(onehot[h][:, :, :], along(iotaB[:, :], 1, UT), along(cur[h][:, :], 2, P),
                                       ALU.is_equal).then_inc(onehot_ready[h], 1)
                                    v.tensor_scalar(cur[h][:, :], cur[h][:, :], -float(P), None, ALU.add)\
                                        .then_inc(cur_moved[h], 1)
                                    begin = w * P
                                dve.wait_ge(added[h], done)
                                dve.wait_ge(added[1 - h], i * W + ((W if h else 0) + 1 + NPAIR * W * k))
                                dve.wait_ge(summed[h], done + 1)
                                span = acc[0:M, bass.ds(begin, P)]
                                tt(span, span, sums[h][0:M, :], ALU.add).then_inc(added[h], 1)

                            over_windows(dve, W, window)
                    ch.leave(NPAIR)

                def clear_sums():
                    v.memset(acc[:, :], 0.0)

                with dve.Fori(0, NNG) as j:
                    ch.enter(j, NORM_CHAIN)
                    norm(0, j)
                ch.leave(NNG)
                edges(SAGE0)

                dve.wait_ge(hist_summed, NG + 1)
                v.tensor_scalar(hist[0:1, 0:1], hist[0:1, 0:1], -float(NG * GE - E), None, ALU.add)\
                    .then_inc(hist_added, 1)
                dve.wait_ge(hist_T, 1)
                v.tensor_scalar(degS[:, :], psC[:, 0:NB], 1.0, None, ALU.add).then_inc(deg_ready, 1)
                dve.wait_ge(deg_root, 1)
                v.reciprocal(degS[:, :], degS[:, :]).then_inc(deg_done, 1)
                with dve.Fori(0, NNG) as j:
                    ch.enter(j, 3)
                    held(dve, dve_turns, (node["mixed"], at("mixed", 1, j)))
                    ch.add(v.tensor_scalar(lnS[0][:, :], psD[:, 0:UT], 1.0, None, ALU.max))
                    held(dve, dve_turns, (dve_chain, ch.value()))
                    v.reciprocal(rdeg[:, bass.ds(j * UT, UT)], lnS[0][:, :])
                    ch.add(v.tensor_scalar(ind[:, bass.ds(j * UT, UT)], psD[:, 0:UT], 1.0, None, ALU.min))
                    dve.wait_ge(stored, stores(1, j))
                    dve.wait_ge(node["hid_T"], before("hid_T", 1, j))
                    ch.wait()
                    ch.add(tt(rows[:, :, :], blocks(psA, HID), along(rdeg[:, bass.ds(j * UT, UT)], 2, HID), ALU.mult))
                    ch.wait()
                    tt(rows[:, :, :], rows[:, :, :], blocks(psB, HID), ALU.add).then_inc(node["scaled"], 1)
                ch.leave(NNG)
                clear_sums()
                edges(SAGE1)

                with dve.Fori(0, NNG) as j:
                    ch.enter(j, 2 + NORM_CHAIN + SHEAF_CHAIN)
                    dve.wait_ge(node["mixed"], at("mixed", 2, j))
                    dve.wait_ge(stored, stores(2, j))
                    ch.add(tt(rows[:, :, :], blocks(psA, HID), along(rdeg[:, bass.ds(j * UT, UT)], 2, HID), ALU.mult))
                    ch.wait()
                    tt(rows[:, :, :], rows[:, :, :], blocks(psB, HID), ALU.add).then_inc(node["scaled"], 1)
                    dve.wait_ge(node["outed"], at("outed", 2, j))
                    ch.add(tt(xs(j), xs(j), blocks(psD, C), ALU.add))
                    norm(2, j)
                    dve.wait_ge(node["table_act"], at("table_act", 2, j))
                    tt(rows[:, :, 0:C], blocks(psA, C, P), along(degS[:, bass.ds(j * UT, UT)], 2, C), ALU.mult)\
                        .then_inc(node["table_dve"], 1)
                    dve.wait_ge(node["table_dve"], at("table_dve", 2, j))
                    sheaf(j + 1, rows, rows[:, :, C:C + 2 * H], msg[0][:, :, :], node["loop_msg"])
                ch.leave(NNG)
                dve.wait_ge(node["loop_T_copied"], at("loop_T_copied", 2, NNG - 1))
                edges(SHEAF)

                with dve.Fori(0, NNG) as j:
                    ch.enter(j, 7 + NORM_CHAIN)
                    dve.wait_ge(node["mixed"], at("mixed", 3, j))
                    ch.add(tt(xc[:, :, :], blocks(psA, C), along(degS[:, bass.ds(j * UT, UT)], 2, C), ALU.mult))
                    ch.wait()
                    v.tensor_scalar(rows[:, :, C:2 * C], xc[:, :, :], 0.0, None, ALU.min).then_inc(node["exp_in"], 1)
                    dve.wait_ge(xr_in, j * 16 + 16)
                    for d in range(D):
                        last = v.tensor_scalar(rows[:, :, d * H:(d + 1) * H], rows[:, :, d * H:(d + 1) * H],
                                               coef[:, d:d + 1], None, ALU.mult)
                    ch.add(last)
                    ch.wait()
                    ch.add(tt(xs(j), xs(j), rows[:, :, 0:C], ALU.add))
                    dve.wait_ge(node["exp_out"], at("exp_out", 3, j))
                    ch.add(v.tensor_scalar(xc[:, :, :], xc[:, :, :], 0.0, None, ALU.max))
                    ch.wait()
                    ch.add(tt(xc[:, :, :], xc[:, :, :], rows[:, :, C:2 * C], ALU.add))
                    ch.wait()
                    ch.add(v.tensor_scalar(xc[:, :, :], xc[:, :, :], -1.0, 1.0, ALU.mult, ALU.add))
                    ch.wait()
                    ch.add(tt(xs(j), xs(j), xc[:, :, :], ALU.add))
                    norm(3, j)
                ch.leave(NNG)
                clear_sums()
                edges(LINEAR)

                with dve.Fori(0, NNG) as j:
                    ch.enter(j, 4 + NORM_CHAIN)
                    dve.wait_ge(node["mixed"], at("mixed", 4, j))
                    ch.add(tt(xc[:, :, :], blocks(psA, C), along(rdeg[:, bass.ds(j * UT, UT)], 2, C), ALU.mult))
                    ch.wait()
                    ch.add(tt(xc[:, :, :], xc[:, :, :], blocks(psB, C), ALU.add))
                    ch.wait()
                    ch.add(tt(xc[:, :, :], xc[:, :, :], along(ind[:, bass.ds(j * UT, UT)], 2, C), ALU.mult))
                    ch.wait()
                    ch.add(tt(xs(j), xs(j), xc[:, :, :], ALU.add))
                    norm(4, j)
                    dve.wait_ge(node["ln"], at("ln", 4, j))
                    tt(rows[:, :, 0:C], hrow[:, :, :], along(bedge[:, :], 1, UT), ALU.add).then_inc(node["biased"], 1)
                ch.leave(NNG)
                dve.wait_ge(node["ln_T_copied"], at("ln_T_copied", 4, NNG - 1))
                edges(GIN)

                with dve.Fori(0, NBN) as m:
                    held(dve, dve_turns, (node["bn_in"], at("bn_in", 5, m)))
                    v.bn_stats(stats[:, bass.ds(m, 1), :].rearrange("p a b -> p (a b)"),
                               hT[0:C, bass.ds(m * BN, BN)]).then_inc(node["bn_stat"], 1)
                dve.wait_ge(node["bn_stat"], at("bn_stat", 5, NBN - 1))
                ch.add(v.bn_aggr(bn[:, 3:5], stats[:, :, :].rearrange("p a b -> p (a b)")))
                ch.wait()
                v.tensor_scalar(bn[:, 4:5], bn[:, 4:5], EPS, None, ALU.add).then_inc(bn_var, 1)
                dve.wait_ge(bn_std, 1)
                ch.add(v.reciprocal(bn[:, 7:8], bn[:, 5:6]))
                ch.wait()
                ch.add(tt(bn[:, 6:7], bn[:, 7:8], bn[:, 1:2], ALU.mult))
                ch.wait()
                ch.add(tt(bn[:, 5:6], bn[:, 3:4], bn[:, 6:7], ALU.mult))
                ch.wait()
                tt(bn[:, 7:8], bn[:, 2:3], bn[:, 5:6], ALU.subtract).then_inc(bn_done, 1)
                with dve.Fori(0, NNG) as j:
                    dve.wait_ge(node["mixed"], at("mixed", 6, j))
                    tt(xs(j), xs(j), blocks(psB, C), ALU.add).then_inc(node["result"], 1)

            by_windows(dve, run)


_NAMES = ["x", "src", "dst", "edge_attr_16", "L0_gnn_W_l0", "L0_gnn_W_r0", "L0_gnn_b_l0", "L0_gnn_W_l1", "L0_gnn_W_r1",
          "L0_gnn_b_l1", "L0_gnn_W_out", "L0_gnn_b_out", "L1_gnn_W1", "L1_gnn_W2", "L1_gnn_epsilons", "L1_gnn_mlp1_w",
          "L1_gnn_mlp1_b", "L1_gnn_mlp2_w", "L1_gnn_mlp2_b", "L2_gnn_W", "L2_gnn_b", "L3_gnn_W_edge", "L3_gnn_b_edge",
          "L3_gnn_W1", "L3_gnn_b1", "L3_gnn_gamma", "L3_gnn_beta", "L3_gnn_W2", "L3_gnn_b2"]


def kernel(**inputs):
    import numpy as _np
    import concourse.bacc as _bacc
    from concourse import mybir as _mybir
    from concourse.bass_utils import run_bass_kernel_spmd as _run

    nc = _bacc.Bacc("TRN2", target_bir_lowering=False, num_devices=1)
    arrays, args = {}, []
    for name in _NAMES:
        a = _np.ascontiguousarray(inputs[name])
        arrays[f"in_{name}"] = a
        args.append(nc.dram_tensor(f"in_{name}", a.shape, _mybir.dt.from_np(a.dtype), kind="ExternalInput").ap())
    out = nc.dram_tensor("result", inputs["x"].shape, _mybir.dt.float32, kind="ExternalOutput").ap()
    gnn_kernel(nc, *args, out)
    r = _run(nc, [arrays], core_ids=[0])
    return r.results[0]["result"]
```

```python
import concourse.bass as bass
from concourse import mybir
from contextlib import ExitStack

F32 = mybir.dt.float32
BF16 = mybir.dt.bfloat16
I32 = mybir.dt.int32
ALU = mybir.AluOpType
ACT = mybir.ActivationFunctionType
AX = mybir.AxisListType

P = 128
UT = 8
GE = UT * P
C = 64
HID = 128
D, H = 4, 16
NPAR = D * (D - 1) // 2
EDIM = 16
EPS = 1e-5

SAGE0, SAGE1, SHEAF, LINEAR, GIN = range(5)


class Chain:

    def __init__(self, eng, sem, before=0):
        self.eng, self.sem, self.before, self.i, self.per, self.n = eng, sem, before, 0, 0, 0

    def enter(self, i, per):
        self.before += self.n
        self.i, self.per, self.n = i, per, 0

    def leave(self, rounds):
        assert self.n == self.per, f"{self.n} instructions are counted in a round, not {self.per}"
        self.before += self.per * rounds
        self.i = self.per = self.n = 0

    def add(self, ins):
        ins.then_inc(self.sem, 1)
        self.n += 1

    def value(self):
        return self.i * self.per + (self.before + self.n)

    def wait(self):
        self.eng.wait_ge(self.sem, self.value())


def gnn_kernel(nc, x, src, dst, edge_attr_16, W_l0, W_r0, b_l0, W_l1, W_r1, b_l1, W_out, b_out,
               sW1, sW2, epsilons, mlp1_w, mlp1_b, mlp2_w, mlp2_b, linW, lin_b,
               W_edge, b_edge, gW1, gb1, gamma, beta, gW2, gb2, out):
    N, E = x.shape[0], src.shape[0]
    NG = 2 * -(-E // (2 * GE))
    NPAIR = NG // 2
    BLOCKS = -(-N // P)
    NNG = -(-(N + P) // GE)
    NB = NNG * UT
    NPAD = NB * P
    PAD_DST = NPAD - 1
    assert PAD_DST >= max(BLOCKS * P, N - 1 + P)
    GFULL, ETAIL = divmod(E, GE)
    NRT = -(-NG * UT // P)
    BN = next(c for c in range(512, 0, -1) if N % c == 0)
    NBN = N // BN

    ctx = ExitStack()
    with ctx:
        ctx.enter_context(nc.allow_non_contiguous_dma(reason="small transposed weights"))

        def sb(name, shape, dt=F32):
            return ctx.enter_context(nc.sbuf_tensor(name, shape, dt))

        def sem(name):
            return ctx.enter_context(nc.semaphore(name))

        def dram(name, shape):
            return nc.dram_tensor(name, shape, F32, kind="Internal").ap()

        tab_h0 = dram("tab_h0", (NPAD, C))
        tab_h1 = dram("tab_h1", (NPAD, HID))
        tab_xr = dram("tab_xr", (NPAD, C))
        tab_sheaf = dram("tab_sheaf", (NPAD, C + 2 * H))
        tab_own = dram("tab_own", (NPAD, 2 * H))
        tab_parts = nc.dram_tensor("tab_parts", (NPAD, 6 * H), BF16, kind="Internal").ap()
        tab_h3 = dram("tab_h3", (NPAD, C))
        tab_h4 = dram("tab_h4", (NPAD, C))
        tab_rel = nc.dram_tensor("tab_rel", (NRT * P, P), BF16, kind="Internal").ap()

        srcI = sb("srcI", [P, NG * UT], I32)
        dstI = sb("dstI", [P, NG * UT], I32)
        rel = sb("rel", [P, NG * UT], BF16)
        shared = sb("shared", [P, max(NG * UT, UT * 5 * H + GE)])
        srcHi, srcLo = (shared[:, :].bitcast(BF16)[:, k * NG * UT:(k + 1) * NG * UT] for k in range(2))
        oneT = shared[:, 0:GE // 2].bitcast(BF16)
        relrow = shared[0:1, GE // 2:GE].bitcast(BF16)
        parts = shared[:, 0:UT * 3 * H].bitcast(BF16).rearrange("p (b f) -> p b f", f=6 * H)
        xfT = shared[0:C + 1, UT * 5 * H:UT * 5 * H + GE]
        rest = shared[:, UT * 3 * H:UT * 5 * H].rearrange("p (b f) -> p b f", f=2 * H)
        ringD = [shared[:, h * UT * 2 * H:(h + 1) * UT * 2 * H].rearrange("p (t f) -> p t f", f=2 * H)
                 for h in range(2)]
        winI = sb("winI", [P, NG], I32)
        acc = sb("acc", [P, NPAD + P])
        hT = sb("hT", [P, NPAD])
        X = sb("X", [P, NB, C])
        degS = sb("degS", [P, NB])
        rdeg = sb("rdeg", [P, NB])
        ind = sb("ind", [P, NB])
        hist = sb("hist", [P, P])
        ident = sb("ident", [P, P])
        iotaB = sb("iotaB", [P, P], BF16)
        ones = sb("ones", [P, P])
        off = sb("off", [P, 1])
        flagI = sb("flagI", [P, 1], I32)

        narrow = sb("narrow", [P, 2 * HID + 6 * C + D + 4 * H])
        column = [0]

        def weight(cols):
            column[0] += cols
            return narrow[0:C, column[0] - cols:column[0]], narrow[C:C + 1, column[0] - cols:column[0]]

        (wl0, bl1r), (wr0, bl0r) = weight(HID), weight(HID)
        wr0b = narrow[0:C + 1, HID:2 * HID]
        at_proj = column[0]
        (proj, b1row) = weight(C + 3 * H)
        projb = narrow[0:C + 1, at_proj:column[0]]
        at_linA = column[0]
        (linA, linbr), (gw2T, gb2r) = weight(C), weight(C)
        linAb, gw2Tb = narrow[0:C + 1, at_linA:at_linA + C], narrow[0:C + 1, at_linA + C:at_linA + 2 * C]
        at_linB = column[0]
        (linB, _), (gw1T, _), (kron, boutr), (w1rep, _), (w2rep, _) = (weight(n) for n in (C, C, C, D, H))
        b2row = narrow[C:C + 1, at_linB:at_linB + 2 * UT * NPAR]
        wl1 = sb("wl1", [HID, HID])
        wr1 = sb("wr1", [HID, HID])
        wout = sb("wout", [HID, C])
        w2bd = sb("w2bd", [P, UT * NPAR])
        w2T = sb("w2T", [H, NPAR])
        weT = sb("weT", [EDIM, C])
        webd = sb("webd", [P, UT * C])
        bedge = sb("bedge", [P, C])
        coef = sb("coef", [P, D])
        bn = sb("bn", [C, 8])

        ixS = [sb(f"ixS{h}", [P, UT], I32) for h in range(2)]
        ixD = [sb(f"ixD{h}", [P, UT], I32) for h in range(2)]
        ringS = [sb(f"ringS{h}", [P, UT, HID]) for h in range(2)]
        pqwin = [sb(f"pqwin{h}", [P, 6 * H], BF16) for h in range(2)]
        qp = sb("qp", [P, UT, 2 * H])
        attr = [sb(f"attr{h}", [P, UT * EDIM]) for h in range(2)]
        onehot = [sb(f"onehot{h}", [P, UT, P]) for h in range(2)]
        cur = [sb(f"cur{h}", [P, UT]) for h in range(2)]
        msg = [sb(f"msg{h}", [P, UT, C]) for h in range(2)]

        hreT = sb("hreT", [P, 2 * P])
        par = [sb(f"par{h}", [P, 2 * UT, NPAR]) for h in range(2)]
        vecs = [sb(f"vecs{h}", [P, 2 * UT, D + 2, D]) for h in range(2)]
        vecA = sb("vecA", [P, 2 * UT, D, D])
        vecB = sb("vecB", [P, 2 * UT, D, D])
        vecN = sb("vecN", [P, 2 * UT, D, D])
        nrel = [sb(f"nrel{h}", [P, UT]) for h in range(2)]
        negp = sb("negp", [P, 1])
        onesB = sb("onesB", [1, P], BF16)
        prod = sb("prod", [P, UT, D, D, D])
        sc = [sb(f"sc{k}", [P, 2 * UT, D]) for k in range(4)]
        rot = sb("rot", [P, UT, D, D])
        stA = sb("stA", [P, GE])
        stH = sb("stH", [P, GE])
        stats = stH[0:C, 0:NBN * 6].rearrange("p (a b) -> p a b", b=6)
        rows = onehot[1]
        xc, hrow = (onehot[0][:, k * 4:(k + 1) * 4, :].rearrange("p b (c f) -> p (b c) f", f=C) for k in range(2))
        sq = ringS[0][:, :, 0:C]
        hi1, lo1 = (stA[:, k * 512:(k + 1) * 512].bitcast(BF16).rearrange("p (t f) -> p t f", f=P) for k in range(2))
        lnS = [sb(f"lnS{k}", [P, UT]) for k in range(4)]

        psA, psB, psC, psD = (ctx.enter_context(nc.psum_tensor(f"ps{k}", [P, GE], F32)) for k in "ABCD")
        sums = [psA[:, 0:P], psA[:, 512:512 + P]]
        preT = psD[:, 0:2 * P]
        parP = psD[:, 512:512 + 2 * UT * NPAR].rearrange("p (x k) -> p x k", k=NPAR)
        edgeP = psC[:, 0:UT * C]
        histP = psD[:, 0:P]

        relF = acc[:, 2 * NG * UT:3 * NG * UT]
        relT = [hreT[:, k * (P // 2):(k + 1) * (P // 2)].bitcast(BF16) for k in range(2)]
        dstF, winF = acc[:, 0:NG * UT], acc[:, NG * UT:NG * UT + NG]

        def blocks(t, width, pitch=None):
            pitch = pitch or width
            return t[:, 0:UT * pitch].rearrange("p (b f) -> p b f", f=pitch)[:, :, 0:width]


        def pair(name):
            return [sem(f"{name}{h}") for h in range(2)]

        padded, indices_in, x_in = sem("padded"), sem("indices_in"), sem("x_in")
        cleared, weights_in, rows_spread = sem("cleared"), sem("weights_in"), sem("rows_spread")
        consts, weights_done, tanh_done = sem("consts"), sem("weights_done"), sem("tanh_done")
        dst_ready, win_summed, rel_ready, off_ready, off_summed = (
            sem(n) for n in ("dst_ready", "win_summed", "rel_ready", "off_ready", "off_summed"))
        prepared, attr_tail = sem("prepared"), sem("attr_tail")
        dve_chain = sem("dve_chain")
        cur_moved = pair("cur_moved")
        sp_turns, pool_turns, pe_turns, act_turns, dve_turns = (
            sem(n) for n in ("sp_turns", "pool_turns", "pe_turns", "act_turns", "dve_turns"))
        stored = sem("stored")

        index_ready, index_dst_ready = pair("index_ready"), pair("index_dst_ready")
        gathered_early, gathered_late, gathered_dst = pair("gathered_early"), pair("gathered_late"), pair("gathered_dst")
        gathered = [gathered_early] * 3 + [gathered_late] * 2
        attr_in = pair("attr_in")
        onehot_ready, summed, added, msg_ready = pair("onehot_ready"), pair("summed"), pair("added"), pair("msg_ready")
        hist_ready, hist_summed = sem("hist_ready"), sem("hist_summed")
        hist_counted = sem("hist_counted")
        hist_added, hist_T, deg_ready, deg_root = sem("hist_added"), sem("hist_T"), sem("deg_ready"), sem("deg_root")
        deg_done = sem("deg_done")

        preT_ready, hid_ready, par_ready = (sem(n) for n in ("preT_ready", "hid_ready", "par_ready"))
        rel_in, rel_spread, oneT_ready, act_chain, qp_ready = (
            sem(n) for n in ("rel_in", "rel_spread", "oneT_ready", "act_chain", "qp_ready"))
        pq_in, xs_copied = pair("pq_in"), pair("xs_copied")
        rel_turned, rel_copied, rel_stored = sem("rel_turned"), sem("rel_copied"), pair("rel_stored")
        par_copied, norm2_ready, norm_ready = sem("par_copied"), sem("norm2_ready"), sem("norm_ready")
        attrT_ready, attrT_copied, edge_ready, pre_relu = (sem(n) for n in ("attrT_ready", "attrT_copied",
                                                                            "edge_ready", "pre_relu"))

        USES = {
            "staged": (1, 2, 3, 4, 5, 6), "mixed": (1, 2, 3, 4, 5, 6), "scaled": (1, 2),
            "hid": (1, 2), "hid_T": (1, 2), "hid_T_copied": (1, 2), "outed": (2,),
            "var": (0, 2, 3, 4), "std": (0, 2, 3, 4), "ln": (0, 2, 3, 4), "ln_T": (0, 2, 3, 4),
            "ln_T_copied": (0, 2, 3, 4), "xf_T": (2,), "xf_T_copied": (2,), "table_mm": (2,), "table_dve": (2,),
            "table_act": (2,), "parts": (2,), "loop_msg": (2,), "loop_T": (2,), "loop_T_copied": (2,),
            "exp_in": (3,), "exp_out": (3,), "biased": (4,), "taken": (3, 4), "bn_in": (5,), "bn_stat": (5,), "result": (6,),
        }
        ROUNDS = (NNG, NNG, NNG, NNG, NNG, NBN, NNG)
        node = {name: sem(name) for name in USES}
        xr_in = sem("xr_in")
        bn_var, bn_std, bn_done = sem("bn_var"), sem("bn_std"), sem("bn_done")
        STORES = (1, 1, 4, 1, 1)
        result_out = sem("result_out")

        def at(name, k, j):
            return j + (2 + sum(ROUNDS[u] for u in USES[name] if u < k))

        def before(name, k, j):
            return j + (1 + sum(ROUNDS[u] for u in USES[name] if u < k))

        def stores(k, j):
            return j * (16 * STORES[k]) + 16 * NNG * sum(STORES[:k])

        def gathers(k, i):
            return i * (16 * UT) + 16 * UT * NPAIR * (k % 3)

        def windows(k, i, W):
            return i * W + (1 + NPAIR * W * k)

        def held(eng, turn, *waits):
            for s, value in waits:
                eng.wait_ge(s, value)
            eng.sem_inc(turn, 1)

        def half(t, i, h):
            return t[:, bass.ds(i * (2 * UT) + h * UT, UT)]

        def skewed(eng, step, enter=None, leave=None):
            step((0, 0), None, None, None)
            step((0, 1), (0, 0), None, None)
            step((1, 0), (0, 1), (0, 0), None)
            with eng.Fori(0, NPAIR - 2) as i:
                if enter:
                    enter(i)
                step((i + 1, 1), (i + 1, 0), (i, 1), (i, 0))
                step((i + 2, 0), (i + 1, 1), (i + 1, 0), (i, 1))
            if leave:
                leave()
            z = NPAIR - 1
            step((z, 1), (z, 0), (z - 1, 1), (z - 1, 0))
            step(None, (z, 1), (z, 0), (z - 1, 1))
            step(None, None, (z, 1), (z, 0))
            step(None, None, None, (z, 1))

        def nth(i, h):
            return i * 2 + (h + 1 + NNG)

        def by_windows(eng, run):
            eng.wait_ge(prepared, 1)
            flag = eng.value_load(flagI[0:1, 0:1], min_val=0, max_val=1)
            with eng.If(flag > 0):
                run(BLOCKS)
            with eng.Else():
                run(1)

        def over_windows(eng, W, step):
            if W == 1:
                step(0)
            else:
                with eng.Fori(0, W) as w:
                    step(w)

        def ahead(eng, first, then):
            first(0)
            with eng.Fori(0, NNG - 1) as j:
                first(j + 1)
                then(j)
            then(NNG - 1)

        nfull, ntail = divmod(N, P)
        block = ctx.enter_context(nc.Block())

        @block.sync
        def _(sp):
            for t, a, n in ((srcI, src, 1), (dstI, dst, 2)):
                sp.wait_ge(padded, n)
                v = t[:, :].rearrange("p (g u) -> p g u", u=UT)
                sp.dma_start(v[:, 0:GFULL, :], a[0:GFULL * GE].rearrange("(g p u) -> p g u", p=P, u=UT))\
                    .then_inc(indices_in, 16)
                q, r = divmod(ETAIL, UT)
                if q:
                    sp.dma_start(v[0:q, GFULL, :],
                                 a[GFULL * GE:GFULL * GE + q * UT].rearrange("(p u) -> p u", u=UT))\
                        .then_inc(indices_in, 16)
                if r:
                    sp.dma_start(v[q:q + 1, GFULL, 0:r],
                                 a[GFULL * GE + q * UT:E].rearrange("(p u) -> p u", p=1)).then_inc(indices_in, 16)
            sp.wait_ge(padded, 3)
            sp.dma_start(X[:, 0:nfull, :], x[0:nfull * P, :].rearrange("(b p) f -> p b f", p=P)).then_inc(x_in, 16)
            if ntail:
                sp.dma_start(X[0:ntail, nfull, :], x[nfull * P:N, :]).then_inc(x_in, 16)

            def same(a, parts, n):
                return bass.AP(tensor=a.tensor, offset=a.offset, ap=[[0, parts], [1, n]])

            def turned(a, rows_, c0, cols):
                return bass.AP(tensor=a.tensor, offset=a.offset + c0,
                               ap=[[1, cols], [a.shape[1], rows_], [1, 1]])

            def cells(t, a, b):
                return t[:, a:b].rearrange("p (f o) -> p f o", o=1)

            sp.wait_ge(cleared, 4)
            loads = [(wl0[:, :], W_l0), (wr0[:, :], W_r0), (wl1[:, :], W_l1), (wr1[:, :], W_r1), (wout[:, :], W_out),
                     (bl0r, same(b_l0, 1, HID)), (bl1r, same(b_l1, 1, HID)), (boutr, same(b_out, 1, C)),
                     (linbr, same(lin_b, 1, C)), (gb2r, same(gb2, 1, C)), (b1row[:, C + H:C + 2 * H], same(mlp1_b, 1, H)),
                     (bedge[:, :], same(b_edge, P, C)), (coef[:, :], same(epsilons, P, D)),
                     (cells(proj, C, C + H), turned(mlp1_w, H, C, C)),
                     (cells(proj, C + H, C + 2 * H), turned(mlp1_w, H, 0, C)),
                     (cells(proj, C + 2 * H, C + 3 * H), turned(mlp1_w, H, C, C)),
                     (cells(w2T, 0, NPAR), turned(mlp2_w, NPAR, 0, H)), (cells(weT, 0, C), turned(W_edge, C, 0, EDIM)),
                     (cells(linA, 0, C), turned(linW, C, 0, C)), (cells(linB, 0, C), turned(linW, C, C, C)),
                     (cells(gw1T, 0, C), turned(gW1, C, 0, C)), (cells(gw2T, 0, C), turned(gW2, C, 0, C))]
            loads += [(bn[:, k:k + 1], a.rearrange("(p o) -> p o", o=1)) for k, a in enumerate((gb1, gamma, beta))]
            loads += [(w1rep[d * H:(d + 1) * H, :],
                       bass.AP(tensor=sW1.tensor, offset=sW1.offset + d * D, ap=[[0, H], [1, D]])) for d in range(D)]
            loads += [(w2rep[d * H:(d + 1) * H, :], sW2) for d in range(D)]
            loads += [(b2row[:, u * NPAR:(u + 1) * NPAR], same(mlp2_b, 1, NPAR)) for u in range(2 * UT)]
            for t, a in loads:
                sp.dma_start(t, a).then_inc(weights_in, 16)
            sp.wait_ge(weights_in, 16 * len(loads))
            for u in range(UT):
                sp.dma_start(w2bd[u * H:(u + 1) * H, u * NPAR:(u + 1) * NPAR], w2T[:, :]).then_inc(rows_spread, 16)
                sp.dma_start(webd[u * EDIM:(u + 1) * EDIM, u * C:(u + 1) * C], weT[:, :]).then_inc(rows_spread, 16)
            for c in range(NRT):
                sp.wait_ge(rel_copied, c + 1)
                n = min(P, NG * UT - c * P)
                sp.dma_start(tab_rel[c * P:c * P + n, :], relT[c % 2][0:n, :]).then_inc(rel_stored[c % 2], 16)
            for k in range(min(2, NRT)):
                sp.wait_ge(rel_stored[k], 16 * ((NRT + 1 - k) // 2))

            def table(t, j):
                return t[bass.ds(j * GE, GE), :].rearrange("(b p) f -> p b f", p=P)

            general = False

            def indices(k, i, h, first=False):
                if not first:
                    held(sp, sp_turns, (gathered[k][h], gathers(k, i)))
                elif k > 0:
                    held(sp, sp_turns, (gathered[k - 1][h], gathers(k - 1, NPAIR)))
                sp.dma_start(ixS[h][:, :], half(srcI, i, h)).then_inc(index_ready[h], 16)
                if k == SHEAF and general:
                    if not first:
                        held(sp, sp_turns, (gathered_dst[h], gathers(0, i)))
                    sp.dma_start(ixD[h][:, :], half(dstI, i, h)).then_inc(index_dst_ready[h], 16)

            def hidden_inputs(i, h):
                held(sp, sp_turns, (rel_spread, nth(i, h) - NNG))
                g = i * 2 + h
                rows_ = tab_rel[g * UT:(g + 1) * UT, :] if isinstance(i, int) else tab_rel[bass.ds(g * UT, UT), :]
                sp.dma_start(relrow, rows_.rearrange("(o t) p -> o (t p)", o=1)).then_inc(rel_in, 16)
                start = sp.value_load(winI[0:1, bass.ds(g, 1)] if not isinstance(i, int) else winI[0:1, g:g + 1],
                                      min_val=0, max_val=N - 1)
                held(sp, sp_turns, (preT_ready, nth(i, h) - 2))
                sp.dma_start(pqwin[h][:, :], tab_parts[bass.ds(start, P), :]).then_inc(pq_in[h], 16)

            def index_pass(k):
                for h in range(2):
                    indices(k, 0, h, first=True)
                with sp.Fori(1, NPAIR) as i:
                    for h in range(2):
                        indices(k, i, h)

            def run(W):
                nonlocal general
                general = W > 1
                with sp.Fori(0, NNG) as j:
                    held(sp, sp_turns, (node["ln"], at("ln", 0, j)))
                    sp.dma_start(table(tab_h0, j), hrow[:, :, :]).then_inc(stored, 16)
                index_pass(SAGE0)
                with sp.Fori(0, NNG) as j:
                    held(sp, sp_turns, (node["hid"], at("hid", 1, j)))
                    sp.dma_start(table(tab_h1, j), rows[:, :, :]).then_inc(stored, 16)
                index_pass(SAGE1)
                with sp.Fori(0, NNG) as j:
                    held(sp, sp_turns, (node["ln"], at("ln", 2, j)))
                    sp.dma_start(table(tab_xr, j), hrow[:, :, :]).then_inc(stored, 16)
                    held(sp, sp_turns, (node["table_dve"], at("table_dve", 2, j)))
                    held(sp, sp_turns, (node["table_act"], at("table_act", 2, j)))
                    sp.dma_start(table(tab_sheaf, j), rows[:, :, 0:C + 2 * H]).then_inc(stored, 16)
                    sp.dma_start(table(tab_own, j), rows[:, :, C + H:C + 3 * H]).then_inc(stored, 16)
                    held(sp, sp_turns, (node["parts"], at("parts", 2, j)))
                    sp.dma_start(table(tab_parts, j), parts[:, :, :]).then_inc(stored, 16)
                if W > 1:
                    index_pass(SHEAF)
                else:
                    sp.wait_ge(stored, stores(SHEAF, NNG))
                    sp.wait_ge(node["loop_T"], at("loop_T", 2, NNG - 1))
                    for h in range(2):
                        indices(SHEAF, 0, h, first=True)
                        hidden_inputs(0, h)
                    with sp.Fori(1, NPAIR) as i:
                        for h in range(2):
                            indices(SHEAF, i, h)
                            hidden_inputs(i, h)
                with sp.Fori(0, NNG) as j:
                    held(sp, sp_turns, (stored, stores(3, 0)))
                    held(sp, sp_turns, (node["ln"], before("ln", 3, j)))
                    held(sp, sp_turns, (node["staged"], at("staged", 3, j)))
                    sp.dma_start(rows[:, :, 0:C], table(tab_xr, j)).then_inc(xr_in, 16)
                    held(sp, sp_turns, (node["ln"], at("ln", 3, j)))
                    sp.dma_start(table(tab_h3, j), hrow[:, :, :]).then_inc(stored, 16)
                index_pass(LINEAR)
                with sp.Fori(0, NNG) as j:
                    held(sp, sp_turns, (node["biased"], at("biased", 4, j)))
                    sp.dma_start(table(tab_h4, j), rows[:, :, 0:C]).then_inc(stored, 16)

                for h in range(2):
                    indices(GIN, 0, h, first=True)
                with sp.Fori(0, NPAIR - 1) as i:
                    for h in range(2):
                        held(sp, sp_turns, (attrT_ready, i * 2 + (h + 1)))
                        sp.dma_start(attr[h][:, :], edge_attr_16[bass.ds(i * (2 * GE) + h * GE, GE), :]
                                     .rearrange("(p u) f -> p (u f)", p=P)).then_inc(attr_in[h], 16)
                    for h in range(2):
                        indices(GIN, i + 1, h)
                for h in range(2):
                    g = NG - 2 + h
                    held(sp, sp_turns, (attrT_ready, g + 1))
                    q, r = divmod(max(0, min(GE, E - g * GE)), UT)
                    if r:
                        sp.dma_start(attr[h][q:q + 1, 0:r * EDIM],
                                     edge_attr_16[g * GE + q * UT:E, :].rearrange("(p u) f -> p (u f)", p=1))\
                            .then_inc(attr_tail, 16)
                        held(sp, sp_turns, (attr_tail, 16))
                    if q:
                        sp.dma_start(attr[h][0:q, :],
                                     edge_attr_16[g * GE:g * GE + q * UT, :].rearrange("(p u) f -> p (u f)", p=q))\
                            .then_inc(attr_in[h], 16)
                    else:
                        sp.sem_inc(attr_in[h], 16)

                with sp.Fori(0, NNG - 1) as j:
                    held(sp, sp_turns, (node["result"], at("result", 6, j)))
                    sp.dma_start(out[bass.ds(j * GE, GE), :].rearrange("(b p) f -> p b f", p=P),
                                 X[:, bass.ds(j * UT, UT), :]).then_inc(result_out, 16)
                held(sp, sp_turns, (node["result"], at("result", 6, NNG - 1)))
                b0 = (NNG - 1) * UT
                if nfull > b0:
                    sp.dma_start(out[b0 * P:nfull * P, :].rearrange("(b p) f -> p b f", p=P),
                                 X[:, b0:nfull, :]).then_inc(result_out, 16)
                if ntail:
                    sp.dma_start(out[nfull * P:N, :], X[0:ntail, nfull, :]).then_inc(result_out, 16)
                held(sp, sp_turns, (result_out, 16 * (NNG - 1 + (nfull > b0) + (ntail > 0))))
                held(sp, sp_turns, (stored, stores(4, NNG)))

            by_windows(sp, run)

        @block.gpsimd
        def _(pool):
            nc.gpsimd.memset(ident[:, :], 0.0).then_inc(pool_turns, 1)
            nc.gpsimd.memset(onehot[0][:, 0, :], 0.0).then_inc(pool_turns, 1)
            pool.wait_ge(pool_turns, 2)
            nc.gpsimd.affine_select(out=ident[:, :], in_=ident[:, :], compare_op=ALU.not_equal, fill=1.0, base=0,
                                    pattern=[[-1, P]], channel_multiplier=1).then_inc(consts, 1)
            nc.gpsimd.affine_select(out=onehot[0][:, 0, :], in_=onehot[0][:, 0, :], compare_op=ALU.not_equal, fill=1.0, base=0,
                                    pattern=[[0, P]], channel_multiplier=1).then_inc(consts, 1)
            nc.gpsimd.iota(iotaB[:, :], pattern=[[1, P]], base=0, channel_multiplier=0,
                           allow_small_or_imprecise_dtypes=True).then_inc(consts, 1)

            nc.gpsimd.iota(negp[:, :], pattern=[[0, 1]], base=0, channel_multiplier=-1,
                           allow_small_or_imprecise_dtypes=True).then_inc(consts, 1)

            def gather(table, slot, index, done):
                pool.indirect_dma_start(slot, None, table[:, :], bass.IndirectOffsetOnAxis(ap=index, axis=0))\
                    .then_inc(done, 16)

            def run(W):
                tables = {SAGE0: (tab_h0, C), SAGE1: (tab_h1, HID), SHEAF: (tab_sheaf, C + 2 * H),
                          LINEAR: (tab_h3, C), GIN: (tab_h4, C)}
                for k, (tab, width) in tables.items():
                    held(pool, pool_turns, (stored, stores(k, NNG)))
                    if k == SHEAF:
                        held(pool, pool_turns, (node["loop_msg"], at("loop_msg", 2, NNG - 1)))
                    with pool.Fori(0, NPAIR) as i:
                        for h in range(2):
                            pool.wait_ge(index_ready[h], i * 16 + 16 * (1 + NPAIR * k))
                            if k == SHEAF:
                                if W > 1:
                                    pool.wait_ge(index_dst_ready[h], i * 16 + 16)
                                held(pool, pool_turns, (xs_copied[h], i + 1), (preT_ready, nth(i, h) - 2))
                            else:
                                held(pool, pool_turns, (summed[h], windows(k, i, W)))
                            for u in range(UT):
                                gather(tab, ringS[h][:, u, 0:width], ixS[h][:, u:u + 1], gathered[k][h])
                                if k == SHEAF and W > 1:
                                    gather(tab_own, ringD[h][:, u, :], ixD[h][:, u:u + 1], gathered_dst[h])

            by_windows(pool, run)

        @block.scalar
        def _(act):
            def copy(out_, in_):
                return nc.scalar.activation(out_, in_, ACT.Copy)

            ac = Chain(act, act_chain)
            for c in range(NRT):
                act.wait_ge(rel_turned, c + 1)
                if c >= 2:
                    act.wait_ge(rel_stored[c % 2], 16 * (c // 2))
                n = min(P, NG * UT - c * P)
                copy(relT[c % 2][0:n, :], psB[0:n, (c % 2) * 512:(c % 2) * 512 + P]).then_inc(rel_copied, 1)
            act.wait_ge(rows_spread, 32 * UT)
            nc.scalar.activation(coef[:, :], coef[:, :], ACT.Tanh).then_inc(tanh_done, 1)

            def hidden(n):
                act.wait_ge(preT_ready, n)
                nc.scalar.activation(hreT[:, :], preT, ACT.Relu).then_inc(hid_ready, 1)

            def parameters(n, h):
                act.wait_ge(par_ready, n)
                t = vecs[h]
                copy(t[:, :, 0, 1:3], parP[:, :, 0:2])
                copy(t[:, :, 0, 3], parP[:, :, 3])
                copy(t[:, :, 4, 2:4], parP[:, :, 2:5:2])
                nc.scalar.activation(t[:, :, 3, 2], parP[:, :, 5], ACT.Copy, scale=-1.0)
                nc.scalar.activation(t[:, :, 5, 1], parP[:, :, 2], ACT.Copy, scale=-1.0)
                copy(par[h][:, :, :], parP).then_inc(par_copied, 1)

            def norms(n):
                act.wait_ge(norm2_ready, n)
                nc.scalar.activation(sc[2][:, :, :], sc[3][:, :, :], ACT.Sqrt).then_inc(norm_ready, 1)

            before_ = ac.n

            def run(W):
                nonlocal ac
                ac = Chain(act, act_chain, before_)

                def std(k, j):
                    act.wait_ge(node["var"], at("var", k, j))
                    nc.scalar.activation(lnS[2][:, :], lnS[1][:, :], ACT.Sqrt).then_inc(node["std"], 1)

                def put(k, j, ready, dest, source, done):
                    held(act, act_turns, (node[ready], at(ready, k, j)))
                    copy(dest, source).then_inc(node[done], 1)

                def stage(k, j, agg, own):
                    cols = bass.ds(j * GE, GE)
                    held(act, act_turns, (added[0], windows(k, 0, W)), (added[1], windows(k, 0, W)),
                         (node["mixed"], before("mixed", k, j)))
                    if own:
                        copy(stH[0:own, :], hT[0:own, cols])
                    copy(stA[0:agg, :], acc[0:agg, cols]).then_inc(node["staged"], 1)

                def edges(k):
                    with act.Fori(0, NPAIR) as i:
                        for h in range(2):
                            n = i * 2 + (h + 1)
                            if k == GIN:
                                act.wait_ge(attrT_ready, n + 2)
                                copy(hreT[:, 0:P], psB[:, 0:P]).then_inc(attrT_copied, 1)
                                act.wait_ge(summed[h], windows(k, i, W))
                                act.wait_ge(pre_relu, n)
                                nc.scalar.activation(msg[h][:, :, :], blocks(stH, C), ACT.Relu)\
                                    .then_inc(msg_ready[h], 1)

                with act.Fori(0, NNG) as j:
                    std(0, j)
                    put(0, j, "ln_T", hT[0:C, bass.ds(j * GE, GE)], psC[0:C, :], "ln_T_copied")

                act.wait_ge(deg_ready, 1)
                nc.scalar.activation(degS[:, :], degS[:, :], ACT.Sqrt).then_inc(deg_root, 1)
                def end1(j):
                    act.wait_ge(node["scaled"], at("scaled", 1, j))
                    nc.scalar.activation(rows[:, :, :], rows[:, :, :], ACT.Relu).then_inc(node["hid"], 1)
                    put(1, j, "hid_T", hT[:, bass.ds(j * GE, GE)], psC[:, :], "hid_T_copied")

                ahead(act, lambda j: stage(1, j, C + 1, C), end1)

                def end2(j, more):
                    act.wait_ge(node["scaled"], at("scaled", 2, j))
                    nc.scalar.activation(rows[:, :, :], rows[:, :, :], ACT.Relu).then_inc(node["hid"], 1)
                    put(2, j, "hid_T", stA[:, :], psC[:, :], "hid_T_copied")
                    std(2, j)
                    put(2, j, "ln_T", stA[0:C, :], psC[0:C, :], "ln_T_copied")
                    put(2, j, "xf_T", xfT[0:C, :], psB[0:C, :], "xf_T_copied")
                    put(2, j, "table_mm", rows[:, :, C:C + 3 * H],
                        psA[:, :].rearrange("p (b f) -> p b f", f=P)[:, :, C:C + 3 * H], "table_act")
                    hidden(j + 1)
                    parameters(j + 1, 0)
                    if more:
                        stage(2, j + 1, HID, HID)
                    norms(j + 1)
                    put(2, j, "loop_T", acc[0:C, bass.ds(j * GE, GE)], psC[0:C, :], "loop_T_copied")

                stage(2, 0, HID, HID)
                with act.Fori(0, NNG - 1) as j:
                    end2(j, True)
                end2(NNG - 1, False)

                def step(hid, vec, mes, add):
                    if vec:
                        i, h = vec
                        n = nth(i, h)
                        held(act, act_turns, (msg_ready[h], i + 1))
                        parameters(n, h)
                    if hid and W == 1:
                        n = nth(*hid)
                        act.wait_ge(rel_spread, n - (NNG - 1))
                        act.wait_ge(preT_ready, n - 1)
                        ac.add(nc.scalar.activation(oneT, psC[:, :], ACT.Abs, bias=negp[:, :]))
                        ac.wait()
                        nc.scalar.activation(oneT, oneT, ACT.Relu, bias=1.0, scale=-1.0).then_inc(oneT_ready, 1)
                    if vec:
                        i, h = vec
                        act.wait_ge(summed[h], windows(SHEAF, i, W))
                        copy(msg[h][:, :, :], ringS[h][:, :, 0:C]).then_inc(xs_copied[h], 1)
                    if hid:
                        i, h = hid
                        held(act, act_turns, (gathered[SHEAF][h], gathers(SHEAF, i + 1)),
                             (preT_ready, nth(i, h) - 1))
                        copy(qp[:, :, :], ringS[h][:, :, C:C + 2 * H]).then_inc(qp_ready, 1)
                    if vec and W == 1:
                        i, h = vec
                        ac.add(nc.scalar.activation(nrel[h][:, :], half(rel, i, h), ACT.Copy, scale=-1.0))
                        ac.wait()
                        for u in range(UT):
                            last = nc.scalar.activation(onehot[h][:, u, :], iotaB[:, :], ACT.Abs,
                                                        bias=nrel[h][:, u:u + 1])
                        ac.add(last)
                    if hid:
                        hidden(nth(*hid))
                    if vec:
                        norms(nth(*vec))
                    if vec and W == 1:
                        ac.wait()
                        nc.scalar.activation(onehot[h][:, :, :], onehot[h][:, :, :], ACT.Relu, bias=1.0,
                                             scale=-1.0).then_inc(onehot_ready[h], 1)

                act.wait_ge(stored, stores(SHEAF, NNG))
                skewed(act, step, lambda i: ac.enter(i, 6 if W == 1 else 0), lambda: ac.leave(NPAIR - 2))
                def end3(j):
                    act.wait_ge(node["exp_in"], at("exp_in", 3, j))
                    nc.scalar.activation(rows[:, :, C:2 * C], rows[:, :, C:2 * C], ACT.Exp).then_inc(node["exp_out"], 1)
                    std(3, j)
                    put(3, j, "ln_T", hT[0:C, bass.ds(j * GE, GE)], psC[0:C, :], "ln_T_copied")

                ahead(act, lambda j: stage(3, j, C, 0), end3)

                def end4(j):
                    std(4, j)
                    put(4, j, "ln_T", acc[0:C, bass.ds(j * GE, GE)], psC[0:C, :], "ln_T_copied")

                ahead(act, lambda j: stage(4, j, C, C), end4)

                edges(GIN)
                with act.Fori(0, NBN) as m:
                    held(act, act_turns, (added[0], windows(5, 0, W)), (added[1], windows(5, 0, W)))
                    copy(stA[0:C, 0:BN], acc[0:C, bass.ds(m * BN, BN)]).then_inc(node["staged"], 1)
                    held(act, act_turns, (node["mixed"], at("mixed", 5, m)))
                    nc.scalar.activation(hT[0:C, bass.ds(m * BN, BN)], psA[0:C, 0:BN], ACT.Identity,
                                         bias=bn[:, 0:1]).then_inc(node["bn_in"], 1)
                act.wait_ge(bn_var, 1)
                nc.scalar.activation(bn[:, 5:6], bn[:, 4:5], ACT.Sqrt).then_inc(bn_std, 1)

                with act.Fori(0, NNG) as j:
                    held(act, act_turns, (bn_done, 1), (node["mixed"], before("mixed", 6, j)),
                         (node["bn_in"], at("bn_in", 5, NBN - 1)))
                    nc.scalar.activation(stA[0:C, :], hT[0:C, bass.ds(j * GE, GE)], ACT.Relu, bias=bn[:, 7:8],
                                         scale=bn[:, 6:7]).then_inc(node["staged"], 1)

            by_windows(act, run)

        @block.tensor
        def _(pe):
            def mm(out_, lhsT, rhs, start=True, stop=True):
                return nc.tensor.matmul(out_, lhsT, rhs, start=start, stop=stop)

            def biased(out_, pairs, bias):
                for n, (lhsT, rhs) in enumerate(pairs):
                    mm(out_, lhsT, rhs, start=(n == 0), stop=False)
                return mm(out_, ones[C:C + 1, :], bias, start=False, stop=True)

            def turn(out_, in_):
                return nc.tensor.transpose(out_, in_, ident[0:in_.shape[0], 0:in_.shape[0]])

            def cut(t, b, parts=P, pitch=P):
                return t[0:parts, b * pitch:(b + 1) * pitch]

            pe.wait_ge(consts, 4)
            pe.wait_ge(dst_ready, 1)
            mm(psA[:, 0:NG], onehot[0][:, 0, :], dstF.rearrange("p (g u) -> p g u", u=UT)[:, :, 0]).then_inc(win_summed, 1)
            pe.wait_ge(rel_ready, 1)
            for c in range(NRT):
                if c >= 2:
                    pe.wait_ge(rel_copied, c - 1)
                n = min(P, NG * UT - c * P)
                turn(psB[0:n, (c % 2) * 512:(c % 2) * 512 + P], relF[:, c * P:c * P + n]).then_inc(rel_turned, 1)
            pe.wait_ge(off_ready, 1)
            mm(psA[:, 512:513], ones[:, :], off[:, :]).then_inc(off_summed, 1)
            pe.wait_ge(rows_spread, 32 * UT)
            pe.wait_ge(weights_done, 1)

            def turned(t, own=None):
                mm(preT[:, t * P:(t + 1) * P], qp[:, t * 4:(t + 1) * 4, :], ident[:, :], stop=False)
                if own is not None:
                    return mm(preT[:, t * P:(t + 1) * P], own[:, t * 4:(t + 1) * 4, :], ident[:, :], start=False)

            def parameters(n):
                held(pe, pe_turns, (hid_ready, n))
                wide = UT * NPAR
                mm(psD[:, 512:512 + 2 * wide], ones[C:C + 1, :], b2row, stop=False)
                for t in range(2):
                    last = mm(psD[:, 512 + t * wide:512 + (t + 1) * wide], hreT[:, t * P:(t + 1) * P], w2bd[:, :],
                              start=False, stop=(t == 1))
                last.then_inc(par_ready, 1)

            def run(W):
                def node_T(k, j, ready, source, width, done):
                    held(pe, pe_turns, (node[ready], at(ready, k, j)))
                    for b in range(UT):
                        last = turn(psC[0:width, b * P:(b + 1) * P], source[:, b, :])
                    last.then_inc(node[done], 1)

                def sum_windows(k, i, h, lhs, M):
                    def window(w):
                        done = i * W + w + (1 + NPAIR * W * k)
                        held(pe, pe_turns, (onehot_ready[h], done), (added[h], done))
                        for u in range(UT):
                            last = mm(sums[h][0:M, :], lhs[:, u, 0:M], onehot[h][:, u, :], start=(u == 0),
                                      stop=(u == UT - 1))
                        last.then_inc(summed[h], 1)

                    over_windows(pe, W, window)

                def edges(k):
                    with pe.Fori(0, NPAIR) as i:
                        for h in range(2):
                            n = i * 2 + (h + 1)
                            if k == GIN:
                                held(pe, pe_turns, (attr_in[h], i * 16 + 16))
                                turn(psB[:, 0:P], attr[h][:, :]).then_inc(attrT_ready, 1)
                                held(pe, pe_turns, (attrT_copied, n))
                                mm(edgeP, hreT[:, 0:P], webd[:, :]).then_inc(edge_ready, 1)
                            if k == GIN:
                                held(pe, pe_turns, (msg_ready[h], i + (2 + NPAIR)))
                                lhs, M = msg[h], C
                            else:
                                held(pe, pe_turns, (gathered[k][h], gathers(k, i + 1)))
                                M = {SAGE0: C + 1, SAGE1: HID, LINEAR: C}[k]
                                lhs = ringS[h]

                            sum_windows(k, i, h, lhs, M)
                            if k == SAGE0:
                                held(pe, pe_turns, (hist_ready, n))
                                for u in range(UT):
                                    last = mm(histP, hi1[:, u, :], lo1[:, u, :], start=(u == 0), stop=(u == UT - 1))
                                last.then_inc(hist_summed, 1)

                with pe.Fori(0, NNG) as j:
                    node_T(0, j, "ln", hrow, C, "ln_T")
                edges(SAGE0)

                pe.wait_ge(node["ln_T_copied"], at("ln_T_copied", 0, NNG - 1))
                pe.wait_ge(hist_added, 1)
                turn(psC[:, 0:P], hist[:, :]).then_inc(hist_T, 1)
                pe.wait_ge(deg_ready, 1)
                def mix1(j):
                    held(pe, pe_turns, (node["staged"], at("staged", 1, j)), (node["scaled"], before("scaled", 1, j)))
                    for b in range(UT):
                        mm(cut(psA, b), cut(stA, b, C), wl0[:, :])
                        mm(cut(psB, b), cut(stH, b, C + 1), wr0b)
                        last = mm(psD[:, b:b + 1], stA[C:C + 1, b * P:(b + 1) * P], ones[C:C + 1, 0:1])
                    last.then_inc(node["mixed"], 1)

                ahead(pe, mix1, lambda j: node_T(1, j, "hid", rows, HID, "hid_T"))
                edges(SAGE1)

                def mix2(j):
                    held(pe, pe_turns, (node["staged"], at("staged", 2, j)),
                         (node["table_act"], before("table_act", 2, j)), (node["table_dve"], before("table_dve", 2, j)))
                    for b in range(UT):
                        mm(cut(psA, b), cut(stA, b), wl1[:, :])
                        last = biased(cut(psB, b), [(cut(stH, b), wr1[:, :])], bl1r)
                    last.then_inc(node["mixed"], 1)

                def end2(j, more):
                    node_T(2, j, "hid", rows, HID, "hid_T")
                    held(pe, pe_turns, (node["hid_T_copied"], at("hid_T_copied", 2, j)))
                    for b in range(UT):
                        last = biased(cut(psD, b, P, C), [(cut(stA, b), wout[:, :])], boutr)
                    last.then_inc(node["outed"], 1)
                    node_T(2, j, "ln", hrow, C, "ln_T")
                    held(pe, pe_turns, (node["ln_T_copied"], at("ln_T_copied", 2, j)))
                    for b in range(2):
                        last = mm(psB[0:C, b * 512:(b + 1) * 512], kron[:, :], stA[0:C, b * 512:(b + 1) * 512])
                    last.then_inc(node["xf_T"], 1)
                    held(pe, pe_turns, (node["xf_T_copied"], at("xf_T_copied", 2, j)))
                    for b in range(UT):
                        last = mm(psA[:, b * P:b * P + C + 3 * H], xfT[:, b * P:(b + 1) * P], projb)
                    last.then_inc(node["table_mm"], 1)
                    held(pe, pe_turns, (qp_ready, j + 1))
                    for t in range(2):
                        last = mm(preT[:, t * P:(t + 1) * P], qp[:, t * 4:(t + 1) * 4, :], ident[:, :])
                    last.then_inc(preT_ready, 1)
                    parameters(j + 1)
                    if more:
                        mix2(j + 1)
                    node_T(2, j, "loop_msg", msg[0], C, "loop_T")

                mix2(0)
                with pe.Fori(0, NNG - 1) as j:
                    end2(j, True)
                end2(NNG - 1, False)

                def step(hid, vec, mes, add):
                    if hid and W == 1:
                        i, h = hid
                        held(pe, pe_turns, (rel_in, i * 32 + (16 * h + 16)))
                        for t in range(2):
                            last = mm(psC[:, t * 512:(t + 1) * 512], onesB[:, :], relrow[:, t * 512:(t + 1) * 512])
                        last.then_inc(rel_spread, 1)
                    if vec:
                        parameters(nth(*vec))
                    if add:
                        i, h = add
                        held(pe, pe_turns, (msg_ready[h], i + 2))
                        sum_windows(SHEAF, i, h, msg[h], C)
                    if hid:
                        i, h = hid
                        n = nth(i, h)
                        if W == 1:
                            held(pe, pe_turns, (qp_ready, n), (oneT_ready, n - NNG), (pq_in[h], i * 16 + 16))
                            for t in range(2):
                                for q in range(4):
                                    u = t * 4 + q
                                    for part in range(3):
                                        mm(preT[q * 2 * H:(q + 1) * 2 * H, t * P:(t + 1) * P],
                                           pqwin[h][:, part * 2 * H:(part + 1) * 2 * H], oneT[:, u * P:(u + 1) * P],
                                           start=(part == 0), stop=False)
                                last = mm(preT[:, t * P:(t + 1) * P], qp[:, t * 4:(t + 1) * 4, :], ident[:, :],
                                          start=False)
                            last.then_inc(preT_ready, 1)
                        else:
                            held(pe, pe_turns, (qp_ready, n), (gathered_dst[h], gathers(0, i + 1)))
                            for t in range(2):
                                last = turned(t, ringD[h])
                            last.then_inc(preT_ready, 1)

                pe.wait_ge(node["loop_T_copied"], at("loop_T_copied", 2, NNG - 1))
                skewed(pe, step)

                def mix3(j):
                    held(pe, pe_turns, (node["staged"], at("staged", 3, j)), (node["taken"], before("taken", 3, j)))
                    for b in range(UT):
                        last = turn(cut(psA, b, P, C), cut(stA, b, C))
                    last.then_inc(node["mixed"], 1)

                ahead(pe, mix3, lambda j: node_T(3, j, "ln", hrow, C, "ln_T"))
                edges(LINEAR)

                def mix4(j):
                    held(pe, pe_turns, (node["staged"], at("staged", 4, j)), (node["taken"], before("taken", 4, j)))
                    for b in range(UT):
                        mm(cut(psA, b, P, C), cut(stA, b, C), linB[:, :])
                        last = mm(cut(psB, b, P, C), cut(stH, b, C + 1), linAb)
                    last.then_inc(node["mixed"], 1)

                ahead(pe, mix4, lambda j: node_T(4, j, "ln", hrow, C, "ln_T"))
                edges(GIN)

                with pe.Fori(0, NBN) as m:
                    held(pe, pe_turns, (node["staged"], at("staged", 5, m)))
                    mm(psA[0:C, 0:BN], gw1T[:, :], stA[0:C, 0:BN]).then_inc(node["mixed"], 1)
                with pe.Fori(0, NNG) as j:
                    held(pe, pe_turns, (node["staged"], at("staged", 6, j)), (node["result"], before("result", 6, j)))
                    for b in range(UT):
                        last = mm(cut(psB, b, P, C), cut(stA, b, C + 1), gw2Tb)
                    last.then_inc(node["mixed"], 1)

            by_windows(pe, run)

        @block.vector
        def _(dve):
            ch = Chain(dve, dve_chain)
            v = nc.vector

            def tt(out_, a, b, op):
                return v.tensor_tensor(out_, a, b, op)

            def along(a, axis, n):
                a = a.unsqueeze(axis)
                shape = list(a.shape)
                shape[axis] = n
                return a.to_broadcast(shape)

            g0 = GFULL * UT
            v.memset(srcI[:, g0:NG * UT], 0).then_inc(padded, 1)
            v.memset(dstI[:, g0:NG * UT], PAD_DST).then_inc(padded, 1)
            v.memset(X[:, nfull:NB, :], 0.0).then_inc(padded, 1)
            v.memset(narrow[C:C + 1, :], 0.0).then_inc(cleared, 1)
            v.memset(w2bd[:, :], 0.0).then_inc(cleared, 1)
            v.memset(webd[:, :], 0.0).then_inc(cleared, 1)
            v.memset(ones[:, :], 1.0)
            v.memset(onesB[:, :], 1.0)
            v.memset(stH[C:C + 1, :], 1.0)
            for h in range(2):
                v.memset(vecs[h][:, :, :, :], 0.0)
            for h in range(2):
                v.memset(ringS[h][:, :, :], 1.0)
                v.memset(attr[h][:, :], 0.0)
            ch.add(v.memset(hist[:, :], 0.0))
            dve.wait_ge(consts, 4)
            ch.wait()
            for h in range(2):
                for slot, place in ((0, 0), (3, 3), (4, 1), (5, 2)):
                    v.memset(vecs[h][:, :, slot, place:place + 1], 1.0)
            v.tensor_copy(proj[:, 0:C], ident[0:C, 0:C]).then_inc(cleared, 1)
            for s in [*node.values(), *summed, *added, *xs_copied, *msg_ready, rel_spread]:
                dve.sem_inc(s, 1)
            dve.sem_inc(attrT_ready, 2)
            dve.sem_inc(hist_summed, 1)

            rem, offs, real = (hT[:, k * NG * UT:(k + 1) * NG * UT] for k in range(3))

            def by_group(a):
                return a.rearrange("p (g u) -> p g u", u=UT)

            dve.wait_ge(indices_in, 16 * 2 * (1 + bool(ETAIL // UT) + bool(ETAIL % UT)))
            v.tensor_copy(dstF, dstI[:, :]).then_inc(dst_ready, 1)
            dve.wait_ge(dst_ready, 1)
            ch.add(v.tensor_scalar(real, dstF, float(N), None, ALU.is_lt))
            dve.wait_ge(win_summed, 1)
            ch.add(v.tensor_scalar(winF, psA[:, 0:NG], float(N - 1), None, ALU.min))
            ch.wait()
            v.tensor_copy(winI[:, :], winF)
            tt(by_group(relF), by_group(dstF), along(winF, 2, UT), ALU.subtract).then_inc(rel_ready, 1)
            ch.add(tt(by_group(rem), by_group(dstF), along(winF, 2, UT), ALU.subtract))
            ch.wait()
            v.tensor_copy(rel[:, :], rem)
            ch.add(v.tensor_scalar(offs, rem, float(P - 1), None, ALU.is_gt))
            ch.wait()
            ch.add(tt(offs, offs, real, ALU.mult))
            ch.add(v.tensor_scalar(rem, rem, 0.0, None, ALU.is_lt))
            ch.wait()
            ch.add(tt(offs, offs, rem, ALU.add))
            ch.wait()
            v.reduce_sum(off[:, :], offs, AX.X).then_inc(off_ready, 1)
            scratch = hT[:, 3 * NG * UT:5 * NG * UT].bitcast(I32)
            v.tensor_single_scalar(scratch[:, 0:NG * UT], srcI[:, :], 7, ALU.logical_shift_right)
            ch.add(v.tensor_single_scalar(scratch[:, NG * UT:2 * NG * UT], srcI[:, :], P - 1, ALU.bitwise_and))
            ch.wait()
            v.tensor_copy(srcHi, scratch[:, 0:NG * UT])
            ch.add(v.tensor_copy(srcLo, scratch[:, NG * UT:2 * NG * UT]))
            dve.wait_ge(rows_spread, 32 * UT)
            tt(linA[:, :], linA[:, :], linB[:, :], ALU.subtract)
            for k in range(D):
                v.tensor_scalar(kron[:, k * H:(k + 1) * H], w2rep[:, :], w1rep[:, k:k + 1], None, ALU.mult)
            dve.wait_ge(tanh_done, 1)
            v.tensor_scalar(coef[:, :], coef[:, :], 1.0, None, ALU.add).then_inc(weights_done, 1)
            ch.wait()
            dve.wait_ge(rel_turned, NRT)
            ch.add(v.memset(hT[:, :], 0.0))
            ch.add(v.memset(acc[:, :], 0.0))
            dve.wait_ge(off_summed, 1)
            v.tensor_scalar(flagI[:, :], psA[:, 512:513], 1.0, None, ALU.min).then_inc(prepared, 1)
            dve.wait_ge(x_in, 16 * (1 + (ntail > 0)))
            dve.wait_ge(weights_done, 1)

            def dot(out_, a):
                return v.reduce_sum(out_, a, AX.X)

            def flat(t):
                return t[:, :, :].rearrange("p x k -> p (x k)")

            def sheaf(vec, mes, adding=None):
                if vec:
                    nv, hv = vec
                    p, t = par[hv], vecs[hv]
                    base, other = t[:, :, 0:4:3, :], t[:, :, 4:6, :]
                if mes:
                    n, h, xs_, out_, done, (low, high) = mes
                    dve.wait_ge(norm_ready, n)
                    ch.add(v.reciprocal(flat(sc[1]), flat(sc[2])))
                    ms = ch.value()
                if vec:
                    dve.wait_ge(par_copied, nv)
                    tt(sc[0][:, :, 0:2], p[:, :, 1:3], along(p[:, :, 5], 2, 2), ALU.mult)
                    ch.add(tt(sc[0][:, :, 2], p[:, :, 2], p[:, :, 0], ALU.mult))
                    vs = ch.value()
                if mes:
                    dve.wait_ge(dve_chain, ms)
                    ch.add(tt(vecN[:, :, :, :], vecs[h][:, :, 0:D, :], along(sc[1][:, :, :], 3, D), ALU.mult))
                    ms = ch.value()
                if vec:
                    dve.wait_ge(dve_chain, vs)
                    tt(t[:, :, 5, 0], sc[0][:, :, 2], p[:, :, 1], ALU.subtract)
                    ch.add(tt(t[:, :, 3, 1], sc[0][:, :, 1], p[:, :, 4], ALU.subtract))
                    vs = ch.value()
                if mes:
                    sides = vecN[:, :, :, :].rearrange("p (t s) v k -> p t s v k", s=2)
                    dve.wait_ge(dve_chain, ms)
                    for a in range(D):
                        last = tt(prod[:, :, a, :, :], along(sides[:, :, 0, a, :], 2, D), sides[:, :, 1, :, :],
                                  ALU.mult)
                    ch.add(last)
                    ms = ch.value()
                if vec:
                    dve.wait_ge(dve_chain, vs)
                    ch.add(tt(sc[0][:, :, 3], t[:, :, 3, 1], p[:, :, 0], ALU.mult))
                    vs = ch.value()
                if mes:
                    dve.wait_ge(dve_chain, ms)
                    ch.add(dot(rot[:, :, :, :].rearrange("p t a b -> p (t a b)"),
                               prod[:, :, :, :, :].rearrange("p t a b k -> p (t a b) k")))
                    ms = ch.value()
                    products = [t_[:, c:c + UT * C].rearrange("p (t a g) -> p t a g", a=D, g=H)
                                for t_, c in ((low, 0), (low, UT * C), (high, 0), (high, UT * C))]

                    def product(b):
                        return tt(products[b], along(rot[:, :, :, b], 3, H),
                                  along(xs_[:, :, b * H:(b + 1) * H], 2, D), ALU.mult)
                if vec:
                    dve.wait_ge(dve_chain, vs)
                    ch.add(tt(sc[0][:, :, 1], sc[0][:, :, 0], sc[0][:, :, 3], ALU.subtract))
                    vs = ch.value()
                if mes:
                    dve.wait_ge(dve_chain, ms)
                    product(0)
                if vec:
                    dve.wait_ge(dve_chain, vs)
                    ch.add(tt(t[:, :, 3, 0], sc[0][:, :, 1], p[:, :, 3], ALU.subtract))
                    vs = ch.value()
                if mes:
                    product(1)
                if vec:
                    dve.wait_ge(dve_chain, vs)
                    tt(vecA[:, :, 0:2, :], base, base, ALU.mult)
                    ch.add(tt(vecA[:, :, 2:4, :], base, other, ALU.mult))
                    vs = ch.value()
                if mes:
                    product(2)
                if vec:
                    dve.wait_ge(dve_chain, vs)
                    ch.add(dot(flat(sc[0]), vecA[:, :, :, :].rearrange("p x v k -> p (x v) k")))
                    vs = ch.value()
                if mes:
                    ch.add(product(3))
                    ms = ch.value()
                if vec:
                    dve.wait_ge(dve_chain, vs)
                    tt(vecB[:, :, 0:2, :], other, along(sc[0][:, :, 0:2], 3, D), ALU.mult)
                    ch.add(tt(vecB[:, :, 2:4, :], base, along(sc[0][:, :, 2:4], 3, D), ALU.mult))
                    vs = ch.value()
                if mes:
                    dve.wait_ge(dve_chain, ms)
                    ch.add(tt(low[:, 0:UT * C], low[:, 0:UT * C], high[:, 0:UT * C], ALU.add))
                if vec:
                    dve.wait_ge(dve_chain, vs)
                    ch.add(tt(t[:, :, 1:3, :], vecB[:, :, 0:2, :], vecB[:, :, 2:4, :], ALU.subtract))
                    vs = ch.value()
                if mes:
                    ch.add(tt(low[:, UT * C:], low[:, UT * C:], high[:, UT * C:], ALU.add))
                    ms = ch.value()
                if vec:
                    dve.wait_ge(dve_chain, vs)
                    ch.add(tt(vecA[:, :, :, :], t[:, :, 0:D, :], t[:, :, 0:D, :], ALU.mult))
                    vs = ch.value()
                if adding:
                    adding()
                if vec:
                    dve.wait_ge(dve_chain, vs)
                    dot(flat(sc[3]), vecA[:, :, :, :].rearrange("p x v k -> p (x v) k")).then_inc(norm2_ready, 1)
                if mes:
                    dve.wait_ge(dve_chain, ms)
                    tt(out_.rearrange("p t f -> p (t f)"), low[:, 0:UT * C], low[:, UT * C:], ALU.add)\
                        .then_inc(done, 1)

            VEC_CHAIN, MES_CHAIN = 10, 7
            start = ch.n

            def run(W):
                nonlocal ch
                ch = Chain(dve, dve_chain, start)

                def xs(j):
                    return X[:, bass.ds(j * UT, UT), :]

                def norm(k, j):
                    held(dve, dve_turns, (dve_chain, ch.value()))
                    ch.add(v.reduce_sum(lnS[0][:, :], xs(j), AX.X))
                    ch.wait()
                    ch.add(v.tensor_scalar(lnS[0][:, :], lnS[0][:, :], 1.0 / C, None, ALU.mult))
                    ch.wait()
                    ch.add(tt(xc[:, :, :], xs(j), along(lnS[0][:, :], 2, C), ALU.subtract))
                    ch.wait()
                    ch.add(tt(sq[:, :, :], xc[:, :, :], xc[:, :, :], ALU.mult))
                    ch.wait()
                    ch.add(v.reduce_sum(lnS[3][:, :], sq[:, :, :], AX.X))
                    ch.wait()
                    v.tensor_scalar(lnS[1][:, :], lnS[3][:, :], 1.0 / C, EPS, ALU.mult, ALU.add)\
                        .then_inc(node["var"], 1)
                    dve.wait_ge(node["std"], at("std", k, j))
                    ch.add(v.reciprocal(lnS[3][:, :], lnS[2][:, :]))
                    dve.wait_ge(stored, {0: stores(0, j), 2: stores(2, j), 3: stores(3, j), 4: stores(4, j)}[k])
                    dve.wait_ge(node["ln_T"], before("ln_T", k, j))
                    ch.wait()
                    v.scalar_tensor_tensor(out=hrow[:, :, :], in0=xc[:, :, :], scalar=0.0,
                                           in1=along(lnS[3][:, :], 2, C), op0=ALU.max, op1=ALU.mult)\
                        .then_inc(node["ln"], 1)

                NORM_CHAIN = 6

                def windows_of(k, i, h, start, make=True):
                    M = {SAGE0: C + 1, SAGE1: HID}.get(k, C)

                    def window(w):
                        done = i * W + w + (1 + NPAIR * W * k)
                        if W == 1:
                            if make:
                                one_hot(k, i, h)
                            begin = start
                        else:
                            dve.wait_ge(summed[h], done)
                            dve.wait_ge(cur_moved[h], i * (W + 1) + w + (1 + NPAIR * (W + 1) * k))
                            tt(onehot[h][:, :, :], along(iotaB[:, :], 1, UT), along(cur[h][:, :], 2, P),
                               ALU.is_equal).then_inc(onehot_ready[h], 1)
                            dve.wait_ge(onehot_ready[h], done)
                            v.tensor_scalar(cur[h][:, :], cur[h][:, :], -float(P), None, ALU.add)\
                                .then_inc(cur_moved[h], 1)
                            begin = w * P
                        dve.wait_ge(added[h], done)
                        dve.wait_ge(added[1 - h], i * W + ((W if h else 0) + 1 + NPAIR * W * k))
                        dve.wait_ge(summed[h], done + 1)
                        span = acc[0:M, bass.ds(begin, P)]
                        tt(span, span, sums[h][0:M, :], ALU.add).then_inc(added[h], 1)

                    if W > 1:
                        held(dve, dve_turns, (summed[h], windows(k, i, W)))
                        v.tensor_copy(cur[h][:, :], half(dstI, i, h)).then_inc(cur_moved[h], 1)
                    over_windows(dve, W, window)

                def one_hot(k, i, h):
                    dve.wait_ge(summed[h], windows(k, i, W))
                    tt(onehot[h][:, :, :], along(iotaB[:, :], 1, UT), along(half(rel, i, h), 2, P),
                       ALU.is_equal).then_inc(onehot_ready[h], 1)

                def window_start(i, h):
                    g = i * 2 + h
                    return dve.value_load(winI[0:1, g:g + 1] if isinstance(i, int) else winI[0:1, bass.ds(g, 1)],
                                          min_val=0, max_val=N - 1) if W == 1 else None

                def rows_free(k):
                    dve.wait_ge(stored, stores(k, NNG))
                    name = {SAGE0: "ln_T", SAGE1: "hid_T", SHEAF: "loop_T"}.get(k, "ln_T")
                    dve.wait_ge(node[name], at(name, k, NNG - 1))

                def edges(k):
                    rows_free(k)
                    with dve.Fori(0, NPAIR) as i:
                        for h in range(2):
                            n = i * 2 + (h + 1)
                            start = window_start(i, h)
                            if k == GIN:
                                dve.wait_ge(gathered[k][h], gathers(k, i + 1))
                                if h:
                                    dve.wait_ge(msg_ready[0], i + (2 + NPAIR))
                                else:
                                    dve.wait_ge(msg_ready[1], i + (1 + NPAIR))
                                dve.wait_ge(edge_ready, n)
                                tt(blocks(stH, C), ringS[h][:, :, 0:C], edgeP.rearrange("p (t f) -> p t f", f=C),
                                   ALU.add).then_inc(pre_relu, 1)
                            if k == SAGE0:
                                dve.wait_ge(hist_summed, n)
                                if W == 1:
                                    one_hot(k, i, h)
                                for t, of in ((hi1, srcHi), (lo1, srcLo)):
                                    last = tt(t, along(iotaB[:, :], 1, UT), along(half(of, i, h), 2, P), ALU.is_equal)
                                last.then_inc(hist_ready, 1)
                            windows_of(k, i, h, start, make=(k != SAGE0))
                            if k == SAGE0:
                                dve.wait_ge(hist_summed, n + 1)
                                tt(hist[:, :], hist[:, :], histP, ALU.add).then_inc(hist_counted, 1)

                def sheaf_pass():
                    rows_free(SHEAF)

                    def step(hid, vec, mes, add):
                        def adding():
                            i, h = add
                            windows_of(SHEAF, i, h, window_start(i, h), make=False)

                        if add and (W > 1 or not mes):
                            adding()
                        if mes:
                            dve.wait_ge(xs_copied[mes[1]], mes[0] + 2)
                        sheaf((nth(*vec), vec[1]) if vec else None,
                              (nth(*mes), mes[1], msg[mes[1]], msg[mes[1]][:, :, :], msg_ready[mes[1]],
                               (stA, stH)) if mes else None,
                              adding if add and mes and W == 1 else None)

                    skewed(dve, step, lambda i: ch.enter(i, 2 * (VEC_CHAIN + MES_CHAIN)), lambda: ch.leave(NPAIR - 2))

                def clear_sums():
                    v.memset(acc[:, :], 0.0)

                with dve.Fori(0, NNG) as j:
                    ch.enter(j, NORM_CHAIN)
                    norm(0, j)
                ch.leave(NNG)
                edges(SAGE0)

                v.memset(xfT[C:C + 1, :], 1.0)

                dve.wait_ge(hist_counted, NG)
                v.tensor_scalar(hist[0:1, 0:1], hist[0:1, 0:1], -float(NG * GE - E), None, ALU.add)\
                    .then_inc(hist_added, 1)
                dve.wait_ge(hist_T, 1)
                v.tensor_scalar(degS[:, :], psC[:, 0:NB], 1.0, None, ALU.add).then_inc(deg_ready, 1)
                dve.wait_ge(deg_root, 1)
                v.reciprocal(degS[:, :], degS[:, :]).then_inc(deg_done, 1)
                with dve.Fori(0, NNG) as j:
                    ch.enter(j, 3)
                    held(dve, dve_turns, (node["mixed"], at("mixed", 1, j)))
                    ch.add(v.tensor_scalar(lnS[0][:, :], psD[:, 0:UT], 1.0, None, ALU.max))
                    held(dve, dve_turns, (dve_chain, ch.value()))
                    v.reciprocal(rdeg[:, bass.ds(j * UT, UT)], lnS[0][:, :])
                    ch.add(v.tensor_scalar(ind[:, bass.ds(j * UT, UT)], psD[:, 0:UT], 1.0, None, ALU.min))
                    dve.wait_ge(stored, stores(1, j))
                    dve.wait_ge(node["hid_T"], before("hid_T", 1, j))
                    ch.wait()
                    ch.add(tt(rows[:, :, :], blocks(psA, HID), along(rdeg[:, bass.ds(j * UT, UT)], 2, HID), ALU.mult))
                    ch.wait()
                    tt(rows[:, :, :], rows[:, :, :], blocks(psB, HID), ALU.add).then_inc(node["scaled"], 1)
                ch.leave(NNG)
                clear_sums()
                edges(SAGE1)

                with dve.Fori(0, NNG) as j:
                    ch.enter(j, 6 + NORM_CHAIN + VEC_CHAIN + MES_CHAIN)
                    dve.wait_ge(node["mixed"], at("mixed", 2, j))
                    dve.wait_ge(stored, stores(2, j))
                    ch.add(tt(rows[:, :, :], blocks(psA, HID), along(rdeg[:, bass.ds(j * UT, UT)], 2, HID), ALU.mult))
                    ch.wait()
                    tt(rows[:, :, :], rows[:, :, :], blocks(psB, HID), ALU.add).then_inc(node["scaled"], 1)
                    dve.wait_ge(node["outed"], at("outed", 2, j))
                    ch.add(tt(xs(j), xs(j), blocks(psD, C), ALU.add))
                    norm(2, j)
                    dve.wait_ge(node["table_act"], at("table_act", 2, j))
                    tt(rows[:, :, 0:C], blocks(psA, C, P), along(degS[:, bass.ds(j * UT, UT)], 2, C), ALU.mult)\
                        .then_inc(node["table_dve"], 1)
                    tt(qp[:, :, :], rows[:, :, C:C + 2 * H], rows[:, :, C + H:C + 3 * H], ALU.add).then_inc(qp_ready, 1)
                    ch.add(v.tensor_copy(parts[:, :, 0:2 * H], rows[:, :, C + H:C + 3 * H]))
                    ch.wait()
                    ch.add(tt(rest[:, :, :], rows[:, :, C + H:C + 3 * H], parts[:, :, 0:2 * H], ALU.subtract))
                    ch.wait()
                    ch.add(v.tensor_copy(parts[:, :, 2 * H:4 * H], rest[:, :, :]))
                    ch.wait()
                    ch.add(tt(rest[:, :, :], rest[:, :, :], parts[:, :, 2 * H:4 * H], ALU.subtract))
                    ch.wait()
                    v.tensor_copy(parts[:, :, 4 * H:6 * H], rest[:, :, :]).then_inc(node["parts"], 1)
                    dve.wait_ge(node["table_dve"], at("table_dve", 2, j))
                    sheaf((j + 1, 0), None)
                    sheaf(None, (j + 1, 0, rows, msg[0][:, :, :], node["loop_msg"],
                                 [flat(t) for t in ringS]))
                ch.leave(NNG)
                dve.wait_ge(node["loop_T_copied"], at("loop_T_copied", 2, NNG - 1))
                sheaf_pass()

                with dve.Fori(0, NNG) as j:
                    ch.enter(j, 6 + NORM_CHAIN)
                    dve.wait_ge(node["mixed"], at("mixed", 3, j))
                    dve.wait_ge(node["ln"], before("ln", 3, j))
                    tt(xc[:, :, :], blocks(psA, C), along(degS[:, bass.ds(j * UT, UT)], 2, C), ALU.mult)\
                        .then_inc(node["taken"], 1)
                    dve.wait_ge(node["taken"], at("taken", 3, j))
                    v.tensor_scalar(rows[:, :, C:2 * C], xc[:, :, :], 0.0, None, ALU.min).then_inc(node["exp_in"], 1)
                    dve.wait_ge(xr_in, j * 16 + 16)
                    for d in range(D):
                        last = v.tensor_scalar(rows[:, :, d * H:(d + 1) * H], rows[:, :, d * H:(d + 1) * H],
                                               coef[:, d:d + 1], None, ALU.mult)
                    ch.add(last)
                    ch.wait()
                    ch.add(tt(xs(j), xs(j), rows[:, :, 0:C], ALU.add))
                    dve.wait_ge(node["exp_out"], at("exp_out", 3, j))
                    ch.add(v.tensor_scalar(xc[:, :, :], xc[:, :, :], 0.0, None, ALU.max))
                    ch.wait()
                    ch.add(tt(xc[:, :, :], xc[:, :, :], rows[:, :, C:2 * C], ALU.add))
                    ch.wait()
                    ch.add(v.tensor_scalar(xc[:, :, :], xc[:, :, :], -1.0, 1.0, ALU.mult, ALU.add))
                    ch.wait()
                    ch.add(tt(xs(j), xs(j), xc[:, :, :], ALU.add))
                    norm(3, j)
                ch.leave(NNG)
                clear_sums()
                v.memset(stH[C:C + 1, :], 1.0)
                edges(LINEAR)

                with dve.Fori(0, NNG) as j:
                    ch.enter(j, 3 + NORM_CHAIN)
                    dve.wait_ge(node["mixed"], at("mixed", 4, j))
                    dve.wait_ge(node["ln"], before("ln", 4, j))
                    ch.add(tt(xc[:, :, :], blocks(psA, C), along(rdeg[:, bass.ds(j * UT, UT)], 2, C), ALU.mult))
                    ch.wait()
                    tt(xc[:, :, :], xc[:, :, :], blocks(psB, C), ALU.add).then_inc(node["taken"], 1)
                    dve.wait_ge(node["taken"], at("taken", 4, j))
                    ch.add(tt(xc[:, :, :], xc[:, :, :], along(ind[:, bass.ds(j * UT, UT)], 2, C), ALU.mult))
                    ch.wait()
                    ch.add(tt(xs(j), xs(j), xc[:, :, :], ALU.add))
                    norm(4, j)
                    dve.wait_ge(node["ln"], at("ln", 4, j))
                    tt(rows[:, :, 0:C], hrow[:, :, :], along(bedge[:, :], 1, UT), ALU.add).then_inc(node["biased"], 1)
                ch.leave(NNG)
                dve.wait_ge(node["ln_T_copied"], at("ln_T_copied", 4, NNG - 1))
                edges(GIN)

                with dve.Fori(0, NBN) as m:
                    held(dve, dve_turns, (node["bn_in"], at("bn_in", 5, m)))
                    v.bn_stats(stats[:, bass.ds(m, 1), :].rearrange("p a b -> p (a b)"),
                               hT[0:C, bass.ds(m * BN, BN)]).then_inc(node["bn_stat"], 1)
                dve.wait_ge(node["mixed"], at("mixed", 5, NBN - 1))
                v.memset(stA[C:C + 1, :], 1.0)
                dve.wait_ge(node["bn_stat"], at("bn_stat", 5, NBN - 1))
                ch.add(v.bn_aggr(bn[:, 3:5], stats[:, :, :].rearrange("p a b -> p (a b)")))
                ch.wait()
                v.tensor_scalar(bn[:, 4:5], bn[:, 4:5], EPS, None, ALU.add).then_inc(bn_var, 1)
                dve.wait_ge(bn_std, 1)
                ch.add(v.reciprocal(bn[:, 7:8], bn[:, 5:6]))
                ch.wait()
                ch.add(tt(bn[:, 6:7], bn[:, 7:8], bn[:, 1:2], ALU.mult))
                ch.wait()
                ch.add(tt(bn[:, 5:6], bn[:, 3:4], bn[:, 6:7], ALU.mult))
                ch.wait()
                tt(bn[:, 7:8], bn[:, 2:3], bn[:, 5:6], ALU.subtract).then_inc(bn_done, 1)
                with dve.Fori(0, NNG) as j:
                    dve.wait_ge(node["mixed"], at("mixed", 6, j))
                    tt(xs(j), xs(j), blocks(psB, C), ALU.add).then_inc(node["result"], 1)

            by_windows(dve, run)


_NAMES = ["x", "src", "dst", "edge_attr_16", "L0_gnn_W_l0", "L0_gnn_W_r0", "L0_gnn_b_l0", "L0_gnn_W_l1", "L0_gnn_W_r1",
          "L0_gnn_b_l1", "L0_gnn_W_out", "L0_gnn_b_out", "L1_gnn_W1", "L1_gnn_W2", "L1_gnn_epsilons", "L1_gnn_mlp1_w",
          "L1_gnn_mlp1_b", "L1_gnn_mlp2_w", "L1_gnn_mlp2_b", "L2_gnn_W", "L2_gnn_b", "L3_gnn_W_edge", "L3_gnn_b_edge",
          "L3_gnn_W1", "L3_gnn_b1", "L3_gnn_gamma", "L3_gnn_beta", "L3_gnn_W2", "L3_gnn_b2"]


def kernel(**inputs):
    import numpy as _np
    import concourse.bacc as _bacc
    from concourse import mybir as _mybir
    from concourse.bass_utils import run_bass_kernel_spmd as _run

    nc = _bacc.Bacc("TRN2", target_bir_lowering=False, num_devices=1)
    arrays, args = {}, []
    for name in _NAMES:
        a = _np.ascontiguousarray(inputs[name])
        arrays[f"in_{name}"] = a
        args.append(nc.dram_tensor(f"in_{name}", a.shape, _mybir.dt.from_np(a.dtype), kind="ExternalInput").ap())
    out = nc.dram_tensor("result", inputs["x"].shape, _mybir.dt.float32, kind="ExternalOutput").ap()
    gnn_kernel(nc, *args, out)
    r = _run(nc, [arrays], core_ids=[0])
    return r.results[0]["result"]
```
